# Optimizing a Trainium2 kernel written in Bass

```python
import numpy as np
import jax
import jax.numpy as jnp

def _softmax(x, axis=-1):
    return jax.nn.softmax(x, axis=axis)

def _gelu(x):
    return jax.nn.gelu(x, approximate=True)

def _silu(x):
    return jax.nn.silu(x)

def _sigmoid(x):
    return jax.nn.sigmoid(x)

def _layernorm(x, axis=-1, eps=1e-05):
    m = jnp.mean(x, axis=axis, keepdims=True)
    v = jnp.var(x, axis=axis, keepdims=True)
    return (x - m) / jnp.sqrt(v + eps)

def _scatter_add(tgt, idx, src, axis=0):
    return tgt.at[idx].add(src)

def _segment_sum(src, seg, n):
    return jax.ops.segment_sum(src, seg, n)
kernel_name = 'mk_adaln_attn_ffn_d1_seqx_r4_a5fdd5'

def setup_inputs(seed: int=0):
    np.random.seed(seed)
    _w = jnp.asarray

    def _rec_inputs():
        import jax
        import jax.numpy as jnp
        _rk = jax.random.key(seed)
        x = -0.000125 + 0.9999 * jax.random.normal(jax.random.fold_in(_rk, 1), (8, 256, 512), jnp.float32)
        _lenS = 256 - jax.random.randint(jax.random.fold_in(_rk, 7), (8,), 0, max(1, 256 // 4) + 1, jnp.int32)
        _lenS2 = 256 - jax.random.randint(jax.random.fold_in(_rk, 8), (8,), 0, max(1, 256 // 4) + 1, jnp.int32)
        cond_2048 = 0.000782532 + 0.100527 * jax.random.normal(jax.random.fold_in(_rk, 11), (8, 512), jnp.float32)
        return (x, cond_2048)
    x, cond_2048 = _rec_inputs()

    def _L0_cond_setup():
        import jax, jax.numpy as jnp
        import numpy as np
        key = jax.random.key(seed)
        k1, k2, k3 = jax.random.split(key, 3)
        B, L, D, K = (4, 1024, 512, 4)
        x = jax.random.normal(k1, (B, L, D), dtype=jnp.float32)
        w = jax.random.normal(k2, (K, 1, D), dtype=jnp.float32) * 0.1
        b = jax.random.normal(k3, (D,), dtype=jnp.float32) * 0.1
        return {'x': x, 'w': w, 'b': b}
    _L0_cond_all = _L0_cond_setup()
    _L0_cond_in = {k: v for k, v in _L0_cond_all.items() if k in ('b',)}
    del _L0_cond_all

    def _L0_attn_setup():
        import jax, jax.numpy as jnp
        import numpy as np
        B, S, D, H = (2, 512, 512, 16)
        HD = D // H
        NEG = jnp.float32(-1000000000.0)
        key = jax.random.key(seed)
        ks = jax.random.split(key, 6)
        slopes = np.array([2 ** (-8.0 * (i + 1) / H) for i in range(H)], dtype=np.float32)
        return {'hidden_states': jax.random.normal(ks[0], (B, S, D), jnp.float32), 'qkv_w': jax.random.normal(ks[1], (3 * D, D), jnp.float32) * (1.0 / np.sqrt(D)), 'qkv_b': jax.random.normal(ks[2], (3 * D,), jnp.float32) * 0.01, 'out_w': jax.random.normal(ks[3], (D, D), jnp.float32) * (1.0 / np.sqrt(D)), 'out_b': jax.random.normal(ks[4], (D,), jnp.float32) * 0.01, 'alibi_slopes': jnp.asarray(slopes)}
    _L0_attn_all = _L0_attn_setup()
    _L0_attn_in = {k: v for k, v in _L0_attn_all.items() if k in ('qkv_w', 'qkv_b', 'out_w', 'out_b', 'alibi_slopes')}
    del _L0_attn_all

    def _L0_cond2_setup():
        import jax, jax.numpy as jnp
        import numpy as np
        import math
        D_MODEL = 256
        NUM_HEAD = 16
        NEG_INF = -1e+30
        key = jax.random.key(seed)
        k_x, k_m, k_q, k_k, k_v = jax.random.split(key, 5)
        B, C, T = (4, D_MODEL, 512)
        x = jax.random.normal(k_x, (B, C, T), dtype=jnp.float32)
        mask = (jax.random.uniform(k_m, (B, T)) < 0.9).astype(jnp.float32)
        limit = math.sqrt(6.0 / (C + C))
        Wq = jax.random.uniform(k_q, (C, C), minval=-limit, maxval=limit, dtype=jnp.float32)
        Wk = jax.random.uniform(k_k, (C, C), minval=-limit, maxval=limit, dtype=jnp.float32)
        Wv = jax.random.uniform(k_v, (C, C), minval=-limit, maxval=limit, dtype=jnp.float32)
        b = jnp.zeros((1,), dtype=jnp.float32)
        return {'x': x, 'mask': mask, 'Wq': Wq, 'Wk': Wk, 'Wv': Wv, 'b': b}
    _L0_cond2_all = _L0_cond2_setup()
    _L0_cond2_in = {k: v for k, v in _L0_cond2_all.items() if k in ('Wq', 'Wk', 'Wv', 'b')}
    del _L0_cond2_all

    def _L0_ffn_setup():
        import jax, jax.numpy as jnp
        import numpy as np
        HIDDEN = 512
        INTER = 2048
        COMPRESSION = 128.9

        def _n_ctrl(out_size, in_size):
            return max(16, int(out_size * in_size / COMPRESSION))

        def _catmull_rom_grid(n_ctrl, n_samples):
            t = np.linspace(0.0, n_ctrl - 1.0, n_samples, dtype=np.float64)
            i = np.clip(np.floor(t).astype(np.int64), 0, n_ctrl - 2)
            f = (t - i).astype(np.float32)
            idx = np.stack([np.clip(i + k, 0, n_ctrl - 1) for k in (-1, 0, 1, 2)], axis=0)
            return (jnp.asarray(idx.astype(np.int32)), jnp.asarray(f))

        def spline_reconstruct(control_points, out_size, in_size):
            n = out_size * in_size
            idx, f = _catmull_rom_grid(control_points.shape[0], n)
            p0, p1, p2, p3 = (control_points[idx[0]], control_points[idx[1]], control_points[idx[2]], control_points[idx[3]])
            f2 = f * f
            f3 = f2 * f
            w = 0.5 * (2.0 * p1 + (p2 - p0) * f + (2.0 * p0 - 5.0 * p1 + 4.0 * p2 - p3) * f2 + (3.0 * p1 - p0 - 3.0 * p2 + p3) * f3)
            return w.reshape(out_size, in_size)
        key = jax.random.key(seed)
        k0, k1, k2, k3 = jax.random.split(key, 4)
        hidden_states = jax.random.normal(k0, (4, 512, HIDDEN), dtype=jnp.float32)
        gate_cp = jax.random.normal(k1, (_n_ctrl(INTER, HIDDEN),), dtype=jnp.float32) * 0.02
        up_cp = jax.random.normal(k2, (_n_ctrl(INTER, HIDDEN),), dtype=jnp.float32) * 0.02
        down_cp = jax.random.normal(k3, (_n_ctrl(HIDDEN, INTER),), dtype=jnp.float32) * 0.02
        return {'hidden_states': hidden_states, 'gate_cp': gate_cp, 'up_cp': up_cp, 'down_cp': down_cp}
    _L0_ffn_all = _L0_ffn_setup()
    _L0_ffn_in = {k: v for k, v in _L0_ffn_all.items() if k in ('gate_cp', 'up_cp', 'down_cp')}
    del _L0_ffn_all
    return {'x': x, 'cond_2048': cond_2048, 'L0_cond_b': _L0_cond_in['b'], 'L0_attn_qkv_w': _L0_attn_in['qkv_w'], 'L0_attn_qkv_b': _L0_attn_in['qkv_b'], 'L0_attn_out_w': _L0_attn_in['out_w'], 'L0_attn_out_b': _L0_attn_in['out_b'], 'L0_attn_alibi_slopes': _L0_attn_in['alibi_slopes'], 'L0_cond2_Wq': _L0_cond2_in['Wq'], 'L0_cond2_Wk': _L0_cond2_in['Wk'], 'L0_cond2_Wv': _L0_cond2_in['Wv'], 'L0_cond2_b': _L0_cond2_in['b'], 'L0_ffn_gate_cp': _L0_ffn_in['gate_cp'], 'L0_ffn_up_cp': _L0_ffn_in['up_cp'], 'L0_ffn_down_cp': _L0_ffn_in['down_cp']}

def reference(x, cond_2048, L0_cond_b, L0_attn_qkv_w, L0_attn_qkv_b, L0_attn_out_w, L0_attn_out_b, L0_attn_alibi_slopes, L0_cond2_Wq, L0_cond2_Wk, L0_cond2_Wv, L0_cond2_b, L0_ffn_gate_cp, L0_ffn_up_cp, L0_ffn_down_cp):
    import jax
    import jax.numpy as jnp

    def _L0_cond_ref(x, w, b):
        import jax, jax.numpy as jnp
        import numpy as np
        'Depthwise causal conv1d, channel-last.\n            x: (B, L, D); w: (K, 1, D); b: (D,). Returns (B, L, D).\n            Matches torch: Conv1d(D, D, K, groups=D, padding=K-1)(x.T)[..., :L].T\n            which is exactly a causal conv (left pad K-1, trim to L).\n            '
        K = w.shape[0]
        D = x.shape[-1]
        y = jax.lax.conv_general_dilated(x, w, window_strides=(1,), padding=[(K - 1, 0)], feature_group_count=D, dimension_numbers=('NWC', 'WIO', 'NWC'))
        return y + b

    def _L0_attn_ref(hidden_states, qkv_w, qkv_b, out_w, out_b, alibi_slopes):
        import jax, jax.numpy as jnp
        import numpy as np
        B, S, D, H = (2, 512, 512, 16)
        HD = D // H
        NEG = jnp.float32(-1000000000.0)
        b, s, d = hidden_states.shape
        qkv = hidden_states @ qkv_w.T + qkv_b
        q, k, v = jnp.split(qkv, 3, axis=-1)
        q = q.reshape(b, s, H, HD)
        k = k.reshape(b, s, H, HD)
        v = v.reshape(b, s, H, HD)
        scale = 1.0 / np.sqrt(HD)
        scores = jnp.einsum('bqhd,bkhd->bhqk', q, k) * scale
        pos = jnp.arange(s)
        rel = (pos[None, :] - pos[:, None]).astype(jnp.float32)
        bias = alibi_slopes[:, None, None] * rel
        causal = pos[None, :] <= pos[:, None]
        scores = jnp.where(causal[None, None], scores + bias[None], NEG)
        attn = jax.nn.softmax(scores, axis=-1)
        out = jnp.einsum('bhqk,bkhd->bqhd', attn, v).reshape(b, s, d)
        out = out @ out_w.T + out_b
        return out

    def _L0_cond2_ref(x, mask, Wq, Wk, Wv, b):
        import jax, jax.numpy as jnp
        import numpy as np
        import math
        D_MODEL = 256
        NUM_HEAD = 16
        NEG_INF = -1e+30
        B, C, T = x.shape
        H = NUM_HEAD
        Dh = C // H

        def proj(W):
            y = jnp.einsum('oc,bct->bto', W, x)
            return y.reshape(B, T, H, Dh).transpose(0, 2, 1, 3)
        Q, K, V = (proj(Wq), proj(Wk), proj(Wv))
        att = jnp.einsum('bhqd,bhkd->bhqk', Q, K) * (1.0 / math.sqrt(Dh))
        att = att + b[0]
        m = mask[:, None, None, :]
        att = att * m + (1.0 - m) * NEG_INF
        att = jax.nn.softmax(att, axis=-1)
        y = jnp.einsum('bhqk,bhkd->bhqd', att, V)
        y = y.transpose(0, 2, 1, 3).reshape(B, T, C)
        return y.transpose(0, 2, 1)

    def _L0_ffn_ref(hidden_states, gate_cp, up_cp, down_cp):
        import jax, jax.numpy as jnp
        import numpy as np
        HIDDEN = 512
        INTER = 2048
        COMPRESSION = 128.9

        def _n_ctrl(out_size, in_size):
            return max(16, int(out_size * in_size / COMPRESSION))

        def _catmull_rom_grid(n_ctrl, n_samples):
            t = np.linspace(0.0, n_ctrl - 1.0, n_samples, dtype=np.float64)
            i = np.clip(np.floor(t).astype(np.int64), 0, n_ctrl - 2)
            f = (t - i).astype(np.float32)
            idx = np.stack([np.clip(i + k, 0, n_ctrl - 1) for k in (-1, 0, 1, 2)], axis=0)
            return (jnp.asarray(idx.astype(np.int32)), jnp.asarray(f))

        def spline_reconstruct(control_points, out_size, in_size):
            n = out_size * in_size
            idx, f = _catmull_rom_grid(control_points.shape[0], n)
            p0, p1, p2, p3 = (control_points[idx[0]], control_points[idx[1]], control_points[idx[2]], control_points[idx[3]])
            f2 = f * f
            f3 = f2 * f
            w = 0.5 * (2.0 * p1 + (p2 - p0) * f + (2.0 * p0 - 5.0 * p1 + 4.0 * p2 - p3) * f2 + (3.0 * p1 - p0 - 3.0 * p2 + p3) * f3)
            return w.reshape(out_size, in_size)
        gate_w = spline_reconstruct(gate_cp, INTER, HIDDEN)
        up_w = spline_reconstruct(up_cp, INTER, HIDDEN)
        down_w = spline_reconstruct(down_cp, HIDDEN, INTER)
        gate = jnp.einsum('bsh,ih->bsi', hidden_states, gate_w)
        up = jnp.einsum('bsh,ih->bsi', hidden_states, up_w)
        inter = jax.nn.silu(gate) * up
        return jnp.einsum('bsi,hi->bsh', inter, down_w)
    x = x + _L0_attn_ref(_L0_cond_ref(x, cond_2048[:, None, :], L0_cond_b), L0_attn_qkv_w, L0_attn_qkv_b, L0_attn_out_w, L0_attn_out_b, L0_attn_alibi_slopes)
    x = x + _L0_ffn_ref(_L0_cond2_ref(x, cond_2048, L0_cond2_Wq, L0_cond2_Wk, L0_cond2_Wv, L0_cond2_b), L0_ffn_gate_cp, L0_ffn_up_cp, L0_ffn_down_cp)
    return x

_drawn_inputs = setup_inputs


def setup_inputs(seed=0):
    import zlib

    import numpy as np

    out = dict(_drawn_inputs(seed))
    spreads = {}
    factors = {'L0_attn_qkv_b': 3.242, 'L0_attn_out_b': 3.575}
    for name, (base, spread) in spreads.items():
        noise = np.random.default_rng([zlib.crc32(name.encode()), seed]).standard_normal(out[name].shape)
        drawn = base * np.exp(spread * noise) if base else spread * noise
        out[name] = jnp.asarray(drawn.astype(out[name].dtype))
    for name, factor in factors.items():
        out[name] = (out[name] * factor).astype(out[name].dtype)
    return out
```

```python
from contextlib import ExitStack

import concourse.bass as bass
from concourse import mybir

ALU = mybir.AluOpType
ACT = mybir.ActivationFunctionType
AX_X = mybir.AxisListType.X
F32 = mybir.dt.float32
F32R = mybir.dt.float32r
BF16 = mybir.dt.bfloat16
U8 = mybir.dt.uint8
I32 = mybir.dt.int32

P = 128
B, L, D = 8, 256, 512
H1, HD = 16, 32
H2, DH = 16, 16
TAPS = 8
INTER, HIDDEN = 2048, 512
N_CTRL = int(INTER * HIDDEN / 128.9)
CT = D // P
LT = L // P
SCALE1 = HD ** -0.5
SCALE2 = DH ** -0.5
NEG1 = -1e9
NEG2 = -1e30
GH = 4
NG = H2 // GH
SLOTS = 3
IT = INTER // P
TB = 512
NTB = B * L // TB
ST = TB // P
NRUN = INTER * HIDDEN // P
NU = NRUN // 512
BASIS = 16
NW = 3

ALIBI = 3 * HD
MAX1 = ALIBI + 4
END1 = MAX1 + 2
BLK = 32
MAX2 = 3 * BLK + DH + 2
END2 = MAX2 + 2

V2_BANKS = (0, 1, 6, 7)
CONV_STEPS = 2 * TAPS

PER_BATCH = {
    "x_loaded": 16, "res_loaded": 16, "mask_loaded": 48, "conv_step": CONV_STEPS, "res_biased": 1,
    "qk1_ready": 8, "qk1_out": 8, "high1": 2, "low1": 2, "stack1": 24 * 16,
    "v1_ready": LT, "v1_out": LT, "s1_ready": H1, "s1_max": H1,
    "max1_turned": 1, "max1_high": 1, "max1_low": 1, "max1_rows": 32,
    "t1_ready": H1 // 2, "p1_out": H1 // 2, "pv1_ready": CT, "inv1_out": CT, "o1_out": CT,
    "proj_ready": LT, "x1_out": LT, "x1_stored": 16,
    "q2_ready": LT, "k2_ready": LT, "q2_out": LT, "k2_out": LT, "high2": 2, "low2": 2,
    "v2_ready": CT, "v2_out": CT, "aug_step": 3, "aug_high": 1, "aug_low": 1, "aug_rows": 32,
    "s2_ready": CT * H2, "s2_max": CT * H2, "max2_turned": NG, "max2_high": NG, "max2_low": NG,
    "max2_rows": 32 * NG, "t2_ready": 2 * CT * NG, "p2_out": 2 * CT * NG, "pv2_step": CT * NG,
    "o2_out": NG, "y_turned": NG, "inv2_out": NG, "y_out": NG, "y_stored": 16,
    "stack2_0": 256, "stack2_1": 256, "stack2_2": 256, "stack2_3": 256,
}
PER_BLOCK = {
    "xr_loaded": 16, "gate_ready": IT, "up_ready": IT, "silu_out": IT, "inter_out": IT,
    "down_done": IT, "acc_out": ST, "stored": 16,
}


def attention_part(nc, psum, y_dram, x1_dram, x_lanes, x_rows, taps, conv_b, qkv_wT, qk_b, v_b, out_wT, out_b,
                   slopes, cond, w2T, att_b, aug_consts, pos):
    with ExitStack() as ctx:
        def sb(name, shape, dt=F32):
            return ctx.enter_context(nc.sbuf_tensor(name, shape, dt))

        def sem(name):
            return ctx.enter_context(nc.semaphore(name))

        S = {name: sem(name) for name in PER_BATCH}

        def at(b, name, count):
            return b * PER_BATCH[name] + count

        qkv_w = sb("qkv_w", [P, CT, 3 * D])
        out_w = sb("out_w", [P, CT, D])
        w2 = sb("w2", [P, 3, LT, L])
        tap = sb("tap", [P, CT, TAPS])
        conv_bias = sb("conv_bias", [P, CT])
        qk_bias = sb("qk_bias", [P, 8])
        v_bias = sb("v_bias", [P, D])
        out_bias = sb("out_bias", [P, D])
        slope = sb("slope", [H1, 1])
        aug_s = sb("aug_s", [2, 3])
        ident = sb("ident", [P, P])
        ident_b = sb("ident_b", [P, P], BF16)
        mask_q = sb("mask_q", [P, 2 * P], BF16)
        mask_k = sb("mask_k", [P, 2 * P], BF16)
        ones = sb("ones", [P, HD])

        h_in = sb("h_in", [P, CT, TAPS - 1 + L])
        h = sb("h", [P, CT, L])
        res = sb("res", [P, LT, D])
        high = sb("high", [P, 2048])
        low = sb("low", [P, 2048])
        alibi = high[0:H1, 0:4 * L].rearrange("h (i n) -> h i n", i=4)
        alibi_t = low[0:H1, 0:2 * L].rearrange("h (i n) -> h i n", i=2)
        pos_rows = low[0:H1, 2 * L:3 * L]
        one_rows = low[0:2, 1024:1024 + 512]
        q1 = sb("q1", [P, H1, L])
        k1 = sb("k1", [P, H1, L])
        v1 = sb("v1", [P, LT, D])
        max1 = sb("max1", [P, H1, LT])
        max1_h = sb("max1_h", [LT * H1, P])
        max1_l = sb("max1_l", [LT * H1, P])
        probs = sb("probs", [P, 2, GH, 512])
        inv1 = sb("inv1", [P, L])
        o1 = sb("o1", [P, CT, L])
        x1 = sb("x1", [P, LT, D])
        mask_row = sb("mask_row", [P, D])
        aug_f = sb("aug_f", [2, D])
        aug_h = sb("aug_h", [2, D])
        aug_l = sb("aug_l", [2, D])
        q2 = sb("q2", [P, SLOTS, GH, D])
        k2 = sb("k2", [P, SLOTS, GH, D])
        v2 = sb("v2", [P, CT, H2, 2 * DH])
        max2 = sb("max2", [P, NG, GH, CT])
        max2_h = sb("max2_h", [GH * CT, 2, P])
        max2_l = sb("max2_l", [GH * CT, 2, P])
        o2 = sb("o2", [P, D])
        inv2 = sb("inv2", [P, 2 * CT, 2, 1])
        y = sb("y", [P, CT, L])

        big_loaded = sem("big_loaded")
        small_loaded = sem("small_loaded")
        pads_zero = sem("pads_zero")
        zeroed = sem("zeroed")
        masks_made = sem("masks_made")
        ones_made = sem("ones_made")
        stacks_clear = sem("stacks_clear")
        alibi_step = sem("alibi_step")
        alibi_done = sem("alibi_done")
        fixed_rows = sem("fixed_rows")
        bias_scaled = sem("bias_scaled")
        N_BIG, N_SMALL, N_FIXED = 5, 8, 9

        block = ctx.enter_context(nc.Block())

        @block.sync
        def _(sp):
            for dst, src in ((tap[:], taps.rearrange("(c p) k -> p c k", p=P)), (conv_bias[:], conv_b),
                             (qk_bias[:], qk_b), (v_bias[:], v_b.partition_broadcast(P)),
                             (out_bias[:], out_b.partition_broadcast(P)), (slope[:], slopes),
                             (aug_s[:, 0:2], aug_consts[:, 0:2]),
                             (pos_rows, pos.partition_broadcast(H1))):
                sp.dma_start(dst, src).then_inc(small_loaded, 16)
            sp.dma_start(aug_s[0:1, 2:3], att_b).then_inc(big_loaded, 16)
            sp.dma_start(aug_s[1:2, 2:3], aug_consts[1:2, 2:3]).then_inc(big_loaded, 16)
            sp.dma_start(qkv_w[:], qkv_wT.rearrange("(c p) n -> p c n", p=P)).then_inc(big_loaded, 16)
            sp.dma_start(out_w[:], out_wT.rearrange("(c p) n -> p c n", p=P)).then_inc(big_loaded, 16)
            sp.dma_start(w2[:].rearrange("p i c n -> p (i c) n"), w2T.rearrange("(m p) n -> p m n", p=P))\
                .then_inc(big_loaded, 16)
            sp.wait_ge(small_loaded, 16 * N_SMALL)
            sp.wait_ge(stacks_clear, 4)
            sp.wait_ge(alibi_done, 4)
            sp.wait_ge(ones_made, 2)
            for i in range(4):
                sp.dma_start(q1[ALIBI + i:ALIBI + i + 1, :, :], alibi[:, i, :]).then_inc(fixed_rows, 16)
            for i in range(2):
                sp.dma_start(k1[ALIBI + i:ALIBI + i + 1, :, :], pos_rows).then_inc(fixed_rows, 16)
            for stack, row in ((q2, DH), (q2, 2 * BLK + DH), (k2, MAX2)):
                sp.dma_start(stack[row:row + 2, :, :, :].rearrange("p s g n -> p (s g) n"),
                             one_rows[:, None, :].broadcast_to([2, SLOTS * GH, 512])).then_inc(fixed_rows, 16)

            def load_mask(src):
                sp.dma_start(mask_row[:], src.partition_broadcast(P)).then_inc(S["mask_loaded"], 16)
                for i in range(2):
                    sp.dma_start(aug_f[i:i + 1, :], src.partition_broadcast(1)).then_inc(S["mask_loaded"], 16)

            sp.wait_ge(pads_zero, 1)
            sp.dma_start(h_in[:, :, TAPS - 1:], x_lanes[B - 1]).then_inc(S["x_loaded"], 16)
            sp.dma_start(res[:], x_rows[B - 1]).then_inc(S["res_loaded"], 16)
            load_mask(cond[B - 1])

            with sp.Fori(0, B) as b:
                def wait(name, count):
                    sp.wait_ge(S[name], at(b, name, count))

                for n, (stack, parts) in enumerate(((q1, (high, low, high)), (k1, (high, high, low)))):
                    wait("high1", n + 1)
                    wait("low1", n + 1)
                    for r, part in enumerate(parts):
                        for e in range(4):
                            sp.dma_start(
                                stack[r * HD:(r + 1) * HD, :, :].rearrange("p (o e) n -> p o e n", e=4)[:, :, e, :],
                                part[e * HD:(e + 1) * HD, n * 1024:(n + 1) * 1024].rearrange("p (o n) -> p o n", o=4)
                            ).then_inc(S["stack1"], 16)
                wait("pv1_ready", CT)
                sp.dma_start(h_in[:, :, TAPS - 1:], x_lanes[b]).then_inc(S["x_loaded"], 16)
                wait("x1_out", LT)
                sp.dma_start(x1_dram[b], x1[:]).then_inc(S["x1_stored"], 16)
                sp.dma_start(res[:], x_rows[b]).then_inc(S["res_loaded"], 16)
                wait("aug_low", 1)
                for r, part in ((0, aug_h), (2, aug_l)):
                    sp.dma_start(k2[r * BLK + DH:r * BLK + DH + 2, :, :, :].rearrange("p s g n -> p (s g) n"),
                                 part[:, None, :].broadcast_to([2, SLOTS * GH, D])).then_inc(S["aug_rows"], 16)
                for g in range(NG):
                    if g == 0:
                        wait("high2", 2)
                        wait("low2", 2)
                    if g >= SLOTS:
                        wait("t2_ready", 2 * CT * (g - SLOTS + 1))
                    for off, stack, parts in ((0, q2, (high, low, high, low)), (1024, k2, (high, high, low, low))):
                        for r, part in enumerate(parts):
                            for e in range(2):
                                row = (2 * g + e) * DH
                                sp.dma_start(
                                    stack[r * BLK:r * BLK + DH, g % SLOTS, :, :]
                                    .rearrange("p (t e) n -> p t e n", e=2)[:, :, e, :],
                                    part[row:row + DH, off:off + 1024].rearrange("p (t n) -> p t n", t=2)
                                ).then_inc(S[f"stack2_{g}"], 16)
                wait("y_out", NG)
                sp.dma_start(y_dram[b], y[:]).then_inc(S["y_stored"], 16)
                wait("x1_stored", 16)
                wait("y_stored", 16)
                load_mask(cond[b])
            for name in ("x_loaded", "res_loaded", "mask_loaded"):
                sp.wait_ge(S[name], at(B, name, PER_BATCH[name]))

        @block.gpsimd
        def _(pool):
            pool.memset(h_in[:], 0.0).then_inc(pads_zero, 1)
            pool.memset(ident[:], 0.0).then_inc(zeroed, 1)
            pool.memset(ident_b[:], 0.0).then_inc(zeroed, 1)
            pool.memset(mask_q[:, 0:P], 0.0).then_inc(zeroed, 1)
            pool.memset(mask_k[:, P:2 * P], 0.0).then_inc(zeroed, 1)
            pool.memset(mask_q[:, P:2 * P], NEG1).then_inc(masks_made, 1)
            pool.memset(mask_k[:, 0:P], NEG1).then_inc(masks_made, 1)
            pool.wait_ge(zeroed, 4)
            for t in (ident, ident_b):
                pool.affine_select(out=t[:], in_=t[:], compare_op=ALU.not_equal, fill=1.0, base=0,
                                   pattern=[[-1, P]], channel_multiplier=1).then_inc(masks_made, 1)
            pool.affine_select(out=mask_q[:, 0:P], in_=mask_q[:, 0:P], compare_op=ALU.is_ge, fill=NEG1, base=0,
                               pattern=[[-1, P]], channel_multiplier=1).then_inc(masks_made, 1)
            pool.affine_select(out=mask_k[:, P:2 * P], in_=mask_k[:, P:2 * P], compare_op=ALU.is_ge, fill=NEG1,
                               base=0, pattern=[[1, P]], channel_multiplier=-1).then_inc(masks_made, 1)
            pool.wait_ge(pads_zero, 1)
            pool.wait_ge(small_loaded, 16 * N_SMALL)
            pool.wait_ge(big_loaded, 16 * N_BIG)

            with pool.Fori(0, B) as b:
                def wait(name, count):
                    pool.wait_ge(S[name], at(b, name, count))

                wait("x_loaded", 16)
                products = v1[:].rearrange("p t (u n) -> p (t u) n", n=L)

                def over(t):
                    return t.broadcast_to([P, CT, L])

                nc.gpsimd.tensor_tensor(h[:], h_in[:, :, 0:L], over(tap[:, :, 0:1]), ALU.mult)\
                    .then_inc(S["conv_step"], 1)
                wait("conv_step", 1)
                nc.gpsimd.tensor_tensor(h[:], h[:], over(conv_bias[:, :, None]), ALU.add).then_inc(S["conv_step"], 1)
                for k in range(1, TAPS):
                    if k > 1:
                        wait("conv_step", 2 * k)
                    nc.gpsimd.tensor_tensor(products, h_in[:, :, k:k + L], over(tap[:, :, k:k + 1]), ALU.mult)\
                        .then_inc(S["conv_step"], 1)
                    wait("conv_step", 2 * k + 1)
                    nc.gpsimd.tensor_tensor(h[:], h[:], products, ALU.add).then_inc(S["conv_step"], 1)
                wait("res_loaded", 16)
                nc.gpsimd.tensor_tensor(res[:], res[:], out_bias[:, None, :].broadcast_to([P, LT, D]), ALU.add)\
                    .then_inc(S["res_biased"], 1)
                wait("mask_loaded", 48)
                for i, op in enumerate((ALU.mult, ALU.add, ALU.mult)):
                    if i:
                        wait("aug_step", i)
                    nc.gpsimd.tensor_tensor(aug_f[:], aug_f[:], aug_s[:, i:i + 1].broadcast_to([2, D]), op)\
                        .then_inc(S["aug_step"], 1)

        @block.scalar
        def _(act):
            act.wait_ge(small_loaded, 16 * N_SMALL)
            act.wait_ge(bias_scaled, 1)
            act.wait_ge(fixed_rows, 16 * N_FIXED)
            with act.Fori(0, B) as b:
                def wait(name, count):
                    act.wait_ge(S[name], at(b, name, count))

                for o in range(8):
                    wait("qk1_ready", o + 1)
                    nc.scalar.activation(low[:, o * L:(o + 1) * L], psum[:, 2 + o % 4, 0:L], ACT.Identity,
                                         bias=qk_bias[:, o:o + 1], scale=SCALE1 if o < 4 else 1.0)\
                        .then_inc(S["qk1_out"], 1)
                wait("max1_high", 1)
                wait("max1_low", 1)
                for i, part in enumerate((max1_h, max1_l)):
                    act.dma_start(q1[MAX1 + i:MAX1 + i + 1, :, :].rearrange("p h (t n) -> p (h t) n", t=LT),
                                  part[:, :]).then_inc(S["max1_rows"], 16)
                for p in range(H1 // 2):
                    g = p // 2
                    wait("t1_ready", p + 1)
                    if g >= 2:
                        wait("pv1_ready", g - 1)
                    nc.scalar.activation(probs[:, g % 2, p % 2 * 2:p % 2 * 2 + 2, :],
                                         psum[:, 2 + p % 2 * 2:4 + p % 2 * 2, :], ACT.Exp).then_inc(S["p1_out"], 1)
                wait("stack1", 24 * 16)
                for t in range(LT):
                    wait("q2_ready", t + 1)
                    nc.scalar.activation(low[:, t * D:(t + 1) * D], psum[:, 2 + t, :], ACT.Identity, scale=SCALE2)\
                        .then_inc(S["q2_out"], 1)

                def max_rows(g):
                    wait("max2_high", g + 1)
                    wait("max2_low", g + 1)
                    for i, part in enumerate((max2_h, max2_l)):
                        act.dma_start(q2[MAX2 + i:MAX2 + i + 1, g % SLOTS, :, :]
                                      .rearrange("p h (t n) -> p (h t) n", t=CT), part[:, g % 2, :])\
                            .then_inc(S["max2_rows"], 16)

                def o2_evac(g):
                    wait("pv2_step", CT * (g + 1))
                    if g:
                        wait("y_turned", g)
                    nc.scalar.activation(o2[:], psum[:, 6, :], ACT.Copy).then_inc(S["o2_out"], 1)

                wait("pv1_ready", CT)
                max_rows(0)
                for g in range(NG):
                    for u in range(2 * CT):
                        kt = u // 2
                        wait("t2_ready", 2 * CT * g + u + 1)
                        if g + kt // 2 >= 1:
                            wait("pv2_step", CT * g + kt - 1)
                        nc.scalar.activation(probs[:, kt % 2, u % 2 * 2:u % 2 * 2 + 2, :],
                                             psum[:, 2 + u % 2 * 2:4 + u % 2 * 2, :], ACT.Exp)\
                            .then_inc(S["p2_out"], 1)
                        if u == 1 and g >= 1:
                            o2_evac(g - 1)
                    if g + 1 < NG:
                        max_rows(g + 1)
                o2_evac(NG - 1)

        @block.vector
        def _(dve):
            for t in (q2, k2):
                nc.vector.memset(t[:], 0.0).then_inc(stacks_clear, 1)
            for t in (q1, k1):
                nc.vector.memset(t[ALIBI:P, :, :], 1.0).then_inc(stacks_clear, 1)
            nc.vector.memset(ones[:], 1.0).then_inc(ones_made, 1)
            nc.vector.memset(one_rows, 1.0).then_inc(ones_made, 1)
            nc.vector.memset(v2[:], 1.0).then_inc(ones_made, 1)
            dve.wait_ge(small_loaded, 16 * N_SMALL)
            nc.vector.tensor_scalar(alibi_t[:, 0, :], pos_rows, 0.0, slope[:, 0:1], ALU.mult, ALU.add)\
                .then_inc(alibi_step, 1)
            nc.vector.tensor_scalar(alibi_t[:, 1, :], pos_rows, slope[:, 0:1], -1.0, ALU.mult, ALU.mult)\
                .then_inc(alibi_step, 1)
            nc.vector.tensor_scalar(qk_bias[:, 0:4], qk_bias[:, 0:4], SCALE1, None, ALU.mult).then_inc(bias_scaled, 1)
            dve.wait_ge(alibi_step, 2)
            for i in range(2):
                nc.vector.tensor_copy(alibi[:, 2 * i, :].bitcast(F32R), alibi_t[:, i, :]).then_inc(alibi_done, 1)
            dve.wait_ge(alibi_done, 2)
            for i in range(2):
                nc.vector.tensor_tensor(alibi[:, 2 * i + 1, :], alibi_t[:, i, :], alibi[:, 2 * i, :], ALU.subtract)\
                    .then_inc(alibi_done, 1)
            dve.wait_ge(ones_made, 3)
            dve.wait_ge(fixed_rows, 16 * N_FIXED)

            with dve.Fori(0, B) as b:
                def wait(name, count):
                    dve.wait_ge(S[name], at(b, name, count))

                def split(half, high_sem, low_sem):
                    cols = slice(half * 1024, (half + 1) * 1024)
                    nc.vector.tensor_copy(high[:, cols].bitcast(F32R), low[:, cols]).then_inc(S[high_sem], 1)
                    wait(high_sem, half + 1)
                    nc.vector.tensor_tensor(low[:, cols], low[:, cols], high[:, cols], ALU.subtract)\
                        .then_inc(S[low_sem], 1)

                wait("qk1_out", 4)
                split(0, "high1", "low1")
                wait("qk1_out", 8)
                split(1, "high1", "low1")
                for t in range(LT):
                    wait("v1_ready", t + 1)
                    nc.vector.tensor_tensor(v1[:, t, :], psum[:, t, :], v_bias[:], ALU.add).then_inc(S["v1_out"], 1)
                for i in range(H1):
                    wait("s1_ready", i + 1)
                    nc.vector.reduce_max(max1[:, i, :], psum[:, i % 2, :].rearrange("p (t n) -> p t n", t=LT), AX_X)\
                        .then_inc(S["s1_max"], 1)
                wait("max1_turned", 1)
                turned = psum[0:LT * H1, 7, 0:P]
                nc.vector.tensor_scalar(max1_h[:].bitcast(F32R), turned, -1.0, None, ALU.mult)\
                    .then_inc(S["max1_high"], 1)
                wait("max1_high", 1)
                nc.vector.scalar_tensor_tensor(out=max1_l[:], in0=turned, scalar=-1.0, in1=max1_h[:],
                                               op0=ALU.mult, op1=ALU.subtract).then_inc(S["max1_low"], 1)
                for g in range(CT):
                    wait("pv1_ready", g + 1)
                    if g:
                        wait("o1_out", g)
                    nc.vector.reciprocal(inv1[:], psum[:, 6 + g % 2, L:2 * L]).then_inc(S["inv1_out"], 1)
                    wait("inv1_out", g + 1)
                    nc.vector.tensor_tensor(o1[:, g, :], psum[:, 6 + g % 2, 0:L], inv1[:], ALU.mult)\
                        .then_inc(S["o1_out"], 1)
                wait("res_biased", 1)
                for t in range(LT):
                    wait("proj_ready", t + 1)
                    nc.vector.tensor_tensor(x1[:, t, :], psum[:, t, :], res[:, t, :], ALU.add)\
                        .then_inc(S["x1_out"], 1)
                wait("aug_step", 3)
                nc.vector.tensor_copy(aug_h[:].bitcast(F32R), aug_f[:]).then_inc(S["aug_high"], 1)
                wait("aug_high", 1)
                nc.vector.tensor_tensor(aug_l[:], aug_f[:], aug_h[:], ALU.subtract).then_inc(S["aug_low"], 1)
                wait("stack1", 24 * 16)
                wait("mask_loaded", 48)
                wait("q2_out", LT)
                split(0, "high2", "low2")
                for t in range(LT):
                    wait("k2_ready", t + 1)
                    nc.vector.tensor_tensor(low[:, (2 + t) * D:(3 + t) * D], psum[:, 4 + t, :], mask_row[:], ALU.mult)\
                        .then_inc(S["k2_out"], 1)
                wait("k2_out", LT)
                split(1, "high2", "low2")
                for t in range(CT):
                    wait("v2_ready", t + 1)
                    nc.vector.tensor_copy(v2[:, t, :, 0:DH],
                                          psum[:, V2_BANKS[t], 0:L].rearrange("p (h d) -> p h d", h=H2))\
                        .then_inc(S["v2_out"], 1)

                def maxima(g, first, end):
                    for n in range(first, end):
                        wait("s2_ready", GH * CT * g + n + 1)
                        nc.vector.reduce_max(max2[:, g, n // CT, n % CT:n % CT + 1], psum[:, n % 2, :], AX_X)\
                            .then_inc(S["s2_max"], 1)

                def turn(g):
                    wait("max2_turned", g + 1)
                    if g >= 2:
                        wait("max2_rows", 32 * (g - 1))
                    rows = psum[0:GH * CT, 7, 0:P]
                    nc.vector.tensor_scalar(max2_h[:, g % 2, :].bitcast(F32R), rows, -1.0, None, ALU.mult)\
                        .then_inc(S["max2_high"], 1)
                    wait("max2_high", g + 1)
                    nc.vector.scalar_tensor_tensor(out=max2_l[:, g % 2, :], in0=rows, scalar=-1.0,
                                                   in1=max2_h[:, g % 2, :], op0=ALU.mult, op1=ALU.subtract)\
                        .then_inc(S["max2_low"], 1)

                def outputs(g):
                    wait("y_turned", g + 1)
                    if g:
                        wait("y_out", g)
                    heads = psum[:, 7, :].rearrange("p (q e d) -> p q e d", e=2, d=2 * DH)
                    nc.vector.reciprocal(inv2[:], heads[:, :, :, DH:DH + 1]).then_inc(S["inv2_out"], 1)
                    wait("inv2_out", g + 1)
                    dst = y[:].rearrange("p c (t x d) -> p (c t) x d", t=2, d=DH)[:, :, 2 * g:2 * g + 2, :]
                    nc.vector.tensor_tensor(dst, heads[:, :, :, 0:DH],
                                            inv2[:].broadcast_to([P, 2 * CT, 2, DH]), ALU.mult)\
                        .then_inc(S["y_out"], 1)

                maxima(0, 0, GH * CT)
                turn(0)
                for g in range(NG):
                    if g + 1 < NG:
                        maxima(g + 1, 0, 12)
                    if g >= 1:
                        outputs(g - 1)
                    if g + 1 < NG:
                        maxima(g + 1, 12, GH * CT)
                        turn(g + 1)
                outputs(NG - 1)

        @block.tensor
        def _(pe):
            pe.wait_ge(big_loaded, 16 * N_BIG)
            pe.wait_ge(masks_made, 6)
            pe.wait_ge(ones_made, 3)
            pe.wait_ge(fixed_rows, 16 * N_FIXED)

            def r(ap):
                return ap.bitcast(F32R)

            with pe.Fori(0, B) as b:
                def wait(name, count):
                    pe.wait_ge(S[name], at(b, name, count))

                wait("conv_step", CONV_STEPS)
                for o in range(8):
                    if o >= 4:
                        wait("qk1_out", o - 3)
                    for c in range(CT):
                        last = nc.tensor.matmul(psum[:, 2 + o % 4, 0:L], qkv_w[:, c, o * P:(o + 1) * P], h[:, c, :],
                                                start=c == 0, stop=c == CT - 1)
                    last.then_inc(S["qk1_ready"], 1)
                for t in range(LT):
                    for c in range(CT):
                        last = nc.tensor.matmul(psum[:, t, :], h[:, c, t * P:(t + 1) * P], qkv_w[:, c, 2 * D:3 * D],
                                                start=c == 0, stop=c == CT - 1)
                    last.then_inc(S["v1_ready"], 1)
                wait("stack1", 24 * 16)
                wait("v1_out", LT)
                for i in range(H1):
                    if i >= 2:
                        wait("s1_max", i - 1)
                    bank = psum[:, i % 2, :]
                    for t in range(LT):
                        nc.tensor.matmul(bank[:, t * L:(t + 1) * L], r(q1[0:MAX1, i, t * P:(t + 1) * P]),
                                         r(k1[0:MAX1, i, :]), start=t == 0, stop=False, skip_group_check=True)
                    nc.tensor.matmul(bank[:, 0:L], ident_b[:], mask_q[:], start=False, stop=False,
                                     skip_group_check=True)
                    nc.tensor.matmul(bank[:, L + P:2 * L], ident_b[:], mask_q[:, 0:P], start=False, stop=True,
                                     skip_group_check=True).then_inc(S["s1_ready"], 1)
                wait("s1_max", H1)
                nc.tensor.transpose(psum[0:LT * H1, 7, 0:P], max1[:].rearrange("p h t -> p (h t)"), ident[:])\
                    .then_inc(S["max1_turned"], 1)

                def values1(g):
                    wait("p1_out", 2 * g + 2)
                    if g == 1:
                        wait("max1_low", 1)
                    elif g >= 2:
                        wait("o1_out", g - 1)
                    for stat, col in ((v1, 0), (None, L)):
                        for kt in range(LT):
                            for e in range(4):
                                lhsT = v1[:, kt, (4 * g + e) * HD:(4 * g + e + 1) * HD] if stat is v1 else ones[:]
                                last = nc.tensor.matmul(
                                    psum[e * HD:(e + 1) * HD, 6 + g % 2, col + kt * P:col + L], lhsT,
                                    probs[:, g % 2, e, kt * L + kt * P:(kt + 1) * L],
                                    start=kt == 0, stop=kt == LT - 1, skip_group_check=True)
                    last.then_inc(S["pv1_ready"], 1)

                wait("max1_rows", 32)
                for p in range(H1 // 2):
                    if p < 2:
                        wait("qk1_out", 8)
                    else:
                        wait("p1_out", p - 1)
                    for e in range(2):
                        i = 2 * p + e
                        bank = psum[:, 2 + p % 2 * 2 + e, :]
                        for t in range(LT):
                            nc.tensor.matmul(bank[:, t * L:(t + 1) * L], r(k1[0:END1, i, t * P:(t + 1) * P]),
                                             r(q1[0:END1, i, :]), start=t == 0, stop=False, skip_group_check=True)
                        nc.tensor.matmul(bank[:, 0:P], ident_b[:], mask_k[:, P:2 * P], start=False, stop=False,
                                         skip_group_check=True)
                        last = nc.tensor.matmul(bank[:, L:2 * L], ident_b[:], mask_k[:], start=False, stop=True,
                                                skip_group_check=True)
                    last.then_inc(S["t1_ready"], 1)
                    if p % 2 == 1 and p >= 3:
                        values1(p // 2 - 1)
                values1(CT - 1)
                wait("s1_max", H1)
                wait("o1_out", CT)
                for t in range(LT):
                    for c in range(CT):
                        last = nc.tensor.matmul(psum[:, t, :], o1[:, c, t * P:(t + 1) * P], out_w[:, c, :],
                                                start=c == 0, stop=c == CT - 1)
                    last.then_inc(S["proj_ready"], 1)
                wait("x1_out", LT)
                wait("p1_out", H1 // 2)
                for i, ready in ((0, "q2_ready"), (1, "k2_ready")):
                    for o in range(LT):
                        for t in range(LT):
                            last = nc.tensor.matmul(psum[:, 2 + 2 * i + o, :], w2[:, i, t, o * P:(o + 1) * P],
                                                    x1[:, t, :], start=t == 0, stop=t == LT - 1)
                        last.then_inc(S[ready], 1)
                for n in range(CT):
                    for t in range(LT):
                        last = nc.tensor.matmul(psum[:, V2_BANKS[n], 0:L],
                                                x1[:, t, n * P:(n + 1) * P], w2[:, 2, t, :],
                                                start=t == 0, stop=t == LT - 1, skip_group_check=True)
                    last.then_inc(S["v2_ready"], 1)

                def scores(g, n):
                    if n == 0:
                        wait(f"stack2_{g}", 256)
                        wait("aug_rows", 32)
                    if g == 0 and n < 2:
                        wait("v2_out", CT)
                    else:
                        wait("s2_max", GH * CT * g + n - 1)
                    slot, e, t = g % SLOTS, n // CT, n % CT
                    nc.tensor.matmul(psum[:, n % 2, :], r(q2[0:MAX2, slot, e, t * P:(t + 1) * P]),
                                     r(k2[0:MAX2, slot, e, :]), start=True, stop=True).then_inc(S["s2_ready"], 1)

                def turn(g):
                    wait("s2_max", GH * CT * (g + 1))
                    if g == 0:
                        wait("o1_out", CT)
                    elif g >= 2:
                        wait("y_out", g - 1)
                    nc.tensor.transpose(psum[0:GH * CT, 7, 0:P], max2[:, g].rearrange("p h t -> p (h t)"), ident[:])\
                        .then_inc(S["max2_turned"], 1)

                def shifted(g, u):
                    if u == 0:
                        wait("max2_rows", 32 * (g + 1))
                    if g == 0 and u < 2:
                        wait("q2_out", LT)
                        wait("k2_out", LT)
                    else:
                        wait("p2_out", 2 * CT * g + u - 1)
                    kt, slot = u // 2, g % SLOTS
                    for e in range(2):
                        i = u % 2 * 2 + e
                        last = nc.tensor.matmul(psum[:, 2 + i, :], r(k2[0:END2, slot, i, kt * P:(kt + 1) * P]),
                                                r(q2[0:END2, slot, i, :]), start=True, stop=True)
                    last.then_inc(S["t2_ready"], 1)

                def values2(g, kt):
                    wait("p2_out", 2 * CT * g + 2 * kt + 2)
                    if kt == 0:
                        if g == 0:
                            wait("o1_out", CT)
                        else:
                            wait("o2_out", g)
                    for e in range(GH):
                        head = (e // 2) * 8 + 2 * g + e % 2
                        last = nc.tensor.matmul(psum[e * BLK:(e + 1) * BLK, 6, :], v2[:, kt, head, :],
                                                probs[:, kt % 2, e, :], start=kt == 0, stop=kt == CT - 1,
                                                skip_group_check=True)
                    last.then_inc(S["pv2_step"], 1)

                def turn_outputs(g):
                    wait("o2_out", g + 1)
                    if g < NG - 1:
                        wait("max2_low", g + 2)
                    else:
                        wait("y_out", g)
                    for t in range(CT):
                        last = nc.tensor.transpose(psum[:, 7, t * P:(t + 1) * P], o2[:, t * P:(t + 1) * P], ident[:])
                    last.then_inc(S["y_turned"], 1)

                for n in range(GH * CT):
                    scores(0, n)
                turn(0)
                for g in range(NG):
                    done = 0
                    for u in range(2 * CT):
                        shifted(g, u)
                        while g + 1 < NG and done < min(GH * CT, 3 * (u + 1)):
                            scores(g + 1, done)
                            done += 1
                        if u == 3 and g >= 1:
                            turn_outputs(g - 1)
                        if u % 2 == 1 and u >= 3:
                            values2(g, u // 2 - 1)
                        if u == 6 and g + 1 < NG:
                            turn(g + 1)
                    values2(g, CT - 1)
                turn_outputs(NG - 1)


def feed_forward_part(nc, psum, y_dram, x1_dram, ctrl, spline_m, spline_r, seg_mask, out):
    with ExitStack() as ctx:
        def sb(name, shape, dt=F32):
            return ctx.enter_context(nc.sbuf_tensor(name, shape, dt))

        def sem(name):
            return ctx.enter_context(nc.semaphore(name))

        S = {name: sem(name) for name in PER_BLOCK}

        def at(b, name, count):
            return b * PER_BLOCK[name] + count

        x1_blocks = x1_dram.rearrange("(n k) p t d -> n p k t d", n=NTB)
        out_blocks = out.rearrange("(n k) p t d -> n p k t d", n=NTB)
        QC = 2048
        NQ = NRUN // QC
        UQ = QC // 512
        w = [sb(f"w_{n}", [P, NRUN]) for n in ("gate", "up", "down")]
        y = sb("y_all", [P, CT, B * L])
        powers = sb("powers", [NW * 32, 2 * NW, P])
        points = sb("points", [NW * 32, 2, QC])
        coefs = sb("coefs", [NW * 32, 2, QC])
        seg_words = sb("seg", [P, 2, NRUN // 4], I32)
        seg = seg_words[:].rearrange("p o n -> p (o n)").bitcast(U8).rearrange("p (o n) -> p o n", o=2)
        silu = sb("silu", [P, 2, TB])
        inter = sb("inter", [P, 2, TB])
        x_res = sb("x_res", [P, ST, D])
        result = sb("result", [P, ST, D])

        y_loaded = sem("y_loaded")
        tables_loaded = sem("tables_loaded")
        points_loaded = [sem(f"points_loaded{i}") for i in range(2)]
        points_scaled = sem("points_scaled")
        segs_ready = sem("segs_ready")
        first_out = sem("first_out")
        second_out = sem("second_out")

        block = ctx.enter_context(nc.Block())

        @block.sync
        def _(sp):
            sp.dma_start(powers[:].rearrange("p a n -> p (a n)"), spline_r).then_inc(tables_loaded, 16)
            for q in range(NQ):
                if q >= 2:
                    sp.wait_ge(segs_ready, NW * UQ * (q - 1))
                sp.dma_start(points[:, q % 2, :], ctrl[:, q * QC:(q + 1) * QC]).then_inc(points_loaded[q % 2], 16)
                sp.dma_start(coefs[:, q % 2, :], spline_m[:, q * QC:(q + 1) * QC]).then_inc(points_loaded[q % 2], 16)
                if q == 0:
                    sp.dma_start(seg_words[:], seg_mask).then_inc(tables_loaded, 16)
                if q == 1:
                    for i in range(B):
                        sp.dma_start(y[:, :, i * L:(i + 1) * L], y_dram[i]).then_inc(y_loaded, 16)
            with sp.Fori(0, NTB) as b:
                sp.dma_start(x_res[:].rearrange("p (k t) d -> p k t d", t=LT), x1_blocks[b]).then_inc(S["xr_loaded"], 16)
                sp.wait_ge(S["acc_out"], at(b, "acc_out", ST))
                sp.dma_start(out_blocks[b], result[:].rearrange("p (k t) d -> p k t d", t=LT)).then_inc(S["stored"], 16)
            sp.wait_ge(S["stored"], at(NTB, "stored", 0))

        @block.tensor
        def _(pe):
            pe.wait_ge(tables_loaded, 32)
            n = 0
            for u in range(NU):
                pe.wait_ge(points_scaled, u // UQ + 1)
                for i in range(NW):
                    if n >= 4:
                        pe.wait_ge(second_out, n - 3)
                    for e in range(2):
                        last = nc.tensor.matmul(psum[:, 2 * (n % 4) + e, :], powers[:, 2 * i + e, :],
                                                points[:, u // UQ % 2, u % UQ * 512:(u % UQ + 1) * 512],
                                                start=True, stop=True)
                    last.then_inc(segs_ready, 1)
                    n += 1
            pe.wait_ge(y_loaded, 16 * B)
            pe.wait_ge(second_out, NW * NU)

            with pe.Fori(0, NTB) as b:
                def wait(name, count):
                    pe.wait_ge(S[name], at(b, name, count))

                def gate_up(it):
                    if it >= 2:
                        wait("inter_out", it - 1)
                    for i, ready in ((0, "gate_ready"), (1, "up_ready")):
                        for c in range(CT):
                            last = nc.tensor.matmul(psum[:, 4 + 2 * (it % 2) + i, :],
                                                    w[i][:, c * INTER + it * P:c * INTER + (it + 1) * P],
                                                    y[:, c, bass.ts(b, TB)], start=c == 0, stop=c == CT - 1)
                        last.then_inc(S[ready], 1)

                def down(it):
                    wait("inter_out", it + 1)
                    for s in range(ST):
                        last = nc.tensor.matmul(psum[:, s, :], inter[:, it % 2, s * P:(s + 1) * P],
                                                w[2][:, it * HIDDEN:(it + 1) * HIDDEN],
                                                start=it == 0, stop=it == IT - 1)
                    last.then_inc(S["down_done"], 1)

                gate_up(0)
                for it in range(1, IT):
                    gate_up(it)
                    down(it - 1)
                down(IT - 1)

        @block.scalar
        def _(act):
            for n in range(NW * NU):
                act.wait_ge(segs_ready, n + 1)
                nc.scalar.activation(w[n % NW][:, n // NW * 512:(n // NW + 1) * 512], psum[:, 2 * (n % 4), :],
                                     ACT.Copy).then_inc(first_out, 1)
            with act.Fori(0, NTB) as b:
                for it in range(IT):
                    act.wait_ge(S["gate_ready"], at(b, "gate_ready", it + 1))
                    if it >= 2:
                        act.wait_ge(S["inter_out"], at(b, "inter_out", it - 1))
                    nc.scalar.activation(silu[:, it % 2, :], psum[:, 4 + 2 * (it % 2), :], ACT.Silu)\
                        .then_inc(S["silu_out"], 1)

        @block.vector
        def _(dve):
            dve.wait_ge(tables_loaded, 32)
            for n in range(NW * NU):
                if n % (NW * UQ) == 0:
                    q = n // (NW * UQ)
                    dve.wait_ge(points_loaded[q % 2], 32 * (q // 2 + 1))
                    nc.vector.tensor_tensor(points[:, q % 2, :], points[:, q % 2, :], coefs[:, q % 2, :], ALU.mult)\
                        .then_inc(points_scaled, 1)
                dve.wait_ge(first_out, n + 1)
                cols = slice(n // NW * 512, (n // NW + 1) * 512)
                nc.vector.copy_predicated(w[n % NW][:, cols], seg[:, 1 if n % NW == 2 else 0, cols],
                                          psum[:, 2 * (n % 4) + 1, :]).then_inc(second_out, 1)
            with dve.Fori(0, NTB) as b:
                def wait(name, count):
                    dve.wait_ge(S[name], at(b, name, count))

                for it in range(IT):
                    wait("silu_out", it + 1)
                    wait("up_ready", it + 1)
                    if it >= 2:
                        wait("down_done", it - 1)
                    nc.vector.tensor_tensor(inter[:, it % 2, :], psum[:, 5 + 2 * (it % 2), :], silu[:, it % 2, :],
                                            ALU.mult).then_inc(S["inter_out"], 1)
                wait("down_done", IT)
                wait("xr_loaded", 16)
                for s in range(ST):
                    nc.vector.tensor_tensor(result[:, s, :], psum[:, s, :], x_res[:, s, :], ALU.add)\
                        .then_inc(S["acc_out"], 1)
                wait("stored", 16)


def block_program(nc, x_lanes, x_rows, taps, conv_b, qkv_wT, qk_b, v_b, out_wT, out_b, slopes, cond, w2T, att_b,
                  aug_consts, pos, ctrl, spline_m, spline_r, seg_mask, out):
    y_dram = nc.dram_tensor("y_scratch", (B, P, CT, L), F32, kind="Internal").ap()
    x1_dram = nc.dram_tensor("x1_scratch", (B, P, LT, D), F32, kind="Internal").ap()
    with nc.psum_tensor("psum", [P, 8, 512], F32) as psum:
        attention_part(nc, psum, y_dram, x1_dram, x_lanes, x_rows, taps, conv_b, qkv_wT, qk_b, v_b, out_wT,
                       out_b, slopes, cond, w2T, att_b, aug_consts, pos)
        feed_forward_part(nc, psum, y_dram, x1_dram, ctrl, spline_m, spline_r, seg_mask, out)


def spline_tables():
    import numpy as np
    n_samples = INTER * HIDDEN
    t = np.linspace(0.0, N_CTRL - 1.0, n_samples, dtype=np.float64)
    seg = np.clip(np.floor(t).astype(np.int64), 0, N_CTRL - 2).reshape(NRUN, P)
    start = seg[:, 0]
    frac = t.reshape(NRUN, P)[:, 0] - start
    step = (N_CTRL - 1.0) / (n_samples - 1)
    crossed = (seg != start[:, None]).astype(np.uint8)
    basis = 0.5 * np.array([[0, 2, 0, 0], [-1, 0, 1, 0], [2, -5, 4, -1], [-1, 3, -3, 1]], np.float64)
    binom = np.array([[1, 0, 0, 0], [1, 1, 0, 0], [1, 2, 1, 0], [1, 3, 3, 1]], np.float64)
    coefs = np.zeros((2, 4, 4, NRUN))
    for e in range(2):
        c = frac - e
        for j in range(4):
            for m in range(j, 4):
                coefs[e, j] += binom[m, j] * c[None, :] ** (m - j) * basis[m][:, None]
    powers = (np.arange(P)[None, :] * step) ** np.arange(4)[:, None]
    place = np.zeros((NW, 2, 4, 4, 2 * NW, P))
    for i in range(NW):
        for e in range(2):
            place[i, e, :, :, 2 * i + e, :] = powers[:, None, :]
    idx = np.zeros((2, 4, NRUN), np.int64)
    for e in range(2):
        for k in range(4):
            idx[e, k] = np.clip(start + e + k - 1, 0, N_CTRL - 1)
    runs = np.arange(NRUN)
    by_inner = runs.reshape(INTER, CT).T.reshape(-1)
    by_outer = runs.reshape(HIDDEN, IT).T.reshape(-1)
    orders = (by_inner, by_inner, by_outer)
    rows = np.concatenate([coefs.reshape(32, NRUN)[:, o] for o in orders]).astype(np.float32)
    masks = np.ascontiguousarray(np.stack([crossed[by_inner].T, crossed[by_outer].T], axis=1))
    picks = [np.broadcast_to(idx[:, None, :, o], (2, 4, 4, NRUN)).reshape(32, NRUN) for o in orders]
    return rows, place.reshape(NW * 32, 2 * NW * P).astype(np.float32), masks, picks


def kernel(**inputs):
    import numpy as np
    import concourse.bacc as bacc
    from concourse.bass_utils import run_bass_kernel_spmd

    a = {k: np.asarray(v) for k, v in inputs.items()}
    rows, powers, masks, picks = spline_tables()
    x = a["x"]
    cond = a["cond_2048"]
    late = np.concatenate([x[1:], x[:1]])
    qkv_w, qkv_b = a["L0_attn_qkv_w"], a["L0_attn_qkv_b"]
    points = np.concatenate([a[n][i] for n, i in zip(("L0_ffn_gate_cp", "L0_ffn_up_cp", "L0_ffn_down_cp"), picks)])
    arrays = {
        "x_lanes": late.transpose(0, 2, 1).reshape(B, CT, P, L).transpose(0, 2, 1, 3),
        "x_rows": late.reshape(B, LT, P, D).transpose(0, 2, 1, 3),
        "taps": cond.T,
        "conv_b": a["L0_cond_b"].reshape(CT, P).T,
        "qkv_wT": qkv_w.T,
        "qk_b": qkv_b[:2 * D].reshape(8, P).T,
        "v_b": qkv_b[2 * D:],
        "out_wT": a["L0_attn_out_w"].T,
        "out_b": a["L0_attn_out_b"],
        "slopes": a["L0_attn_alibi_slopes"].reshape(H1, 1),
        "cond": np.concatenate([cond[1:], cond[:1]]),
        "w2T": np.concatenate([a["L0_cond2_Wq"].T, a["L0_cond2_Wk"].T, a["L0_cond2_Wv"].T]),
        "att_b": a["L0_cond2_b"].reshape(1, 1),
        "aug_consts": np.array([[1, 0, 0], [-1, 1, NEG2]], np.float32),
        "pos": np.arange(L, dtype=np.float32),
        "ctrl": points,
        "spline_m": rows,
        "spline_r": powers,
        "seg_mask": masks.view(np.int32),
    }
    nc = bacc.Bacc("TRN2", target_bir_lowering=False, num_devices=1)
    args, feed = [], {}
    for name, v in arrays.items():
        v = np.ascontiguousarray(v)
        feed[f"in_{name}"] = v
        args.append(nc.dram_tensor(f"in_{name}", v.shape, mybir.dt.from_np(v.dtype), kind="ExternalInput").ap())
    out = nc.dram_tensor("out", (B, P, LT, D), F32, kind="ExternalOutput").ap()
    block_program(nc, *args, out)
    r = run_bass_kernel_spmd(nc, [feed], core_ids=[0])
    got = r.results[0]["out"]
    return got.transpose(0, 2, 1, 3).reshape(B, L, D)
```

```python
from contextlib import ExitStack

import concourse.bass as bass
from concourse import mybir

ALU = mybir.AluOpType
ACT = mybir.ActivationFunctionType
AX_X = mybir.AxisListType.X
F32 = mybir.dt.float32
F32R = mybir.dt.float32r
BF16 = mybir.dt.bfloat16
U8 = mybir.dt.uint8
I32 = mybir.dt.int32

P = 128
B, L, D = 8, 256, 512
H1, HD = 16, 32
H2, DH = 16, 16
TAPS = 8
INTER, HIDDEN = 2048, 512
N_CTRL = int(INTER * HIDDEN / 128.9)
CT = D // P
LT = L // P
SCALE1 = HD ** -0.5
SCALE2 = DH ** -0.5
NEG1 = -1e9
NEG2 = -1e30
GH = 4
NG = H2 // GH
SLOTS = 3
IT = INTER // P
TB = 512
NTB = B * L // TB
ST = TB // P
NRUN = INTER * HIDDEN // P
HALF = NRUN // 2
NUH = HALF // 512
ITH = IT // 2
Y_AT = 6
NW = 3

ALIBI = 3 * HD
MAX1 = ALIBI + 4
END1 = MAX1 + 2
BLK = 32
MAX2 = 3 * BLK
END2 = MAX2 + 2

QUERY_BLOCKS = ((0, False), (2, False), (1, True))
KEY_BLOCKS = ((0, False), (1, False), (2, True))

GS = GH * CT
NS = NG * GS
NP = 2 * CT * NG
LAG = 3
FOLLOW = GS + 8
TURN_AT = GS + 1
OUT_AT = FOLLOW + 2 * (2 * CT + LAG) + 5
N_STEPS = FOLLOW + 2 * (NP + LAG)
QK1_AT = tuple(range(NS + 2, NS + 2 + 3 * 8, 3))
S1_BANKS = (0, 3)
V1_BANKS = (2, 6)
V2_BANKS = (0, 1, 6, 7)
FIRST_LOADS = (3,) + (2,) * (NG - 1)
HEAD_ORDER = (0, 2, 1, 3)
CONV_STEPS = 2 * TAPS

PER_BATCH = {
    "x_loaded": 16, "res_loaded": 16, "mask_loaded": 48, "conv_step": CONV_STEPS, "res_biased": 1,
    "qk1_ready": 8, "qk1_out": 8, "high1": 2, "low1": 2,
    "queries1": 12 * 16, **{f"keys1_{e}": 3 * 16 for e in range(4)},
    "v1_ready": LT, "v1_out": LT, "s1_ready": H1 // 2, "s1_max": H1 // 2,
    "max1_turned": 1, "max1_high": 1, "max1_low": 1, "max1_rows": 32,
    "t1_ready": H1 // 2, "p1_out": H1 // 2, "pv1_ready": CT, "inv1_out": CT, "o1_out": CT,
    "proj_ready": LT, "x1_out": LT, "x1_stored": 16,
    "q2_ready": LT, "k2_ready": LT, "q2_out": LT, "k2_out": LT, "high2": 2, "low2": 2,
    "v2_ready": CT, "v2_out": CT, "aug_step": 3, "aug_high": 1, "aug_low": 1, "aug_rows": 32,
    "s2_ready": CT * H2, "s2_max": CT * H2, "max2_turned": NG, "max2_high": NG, "max2_low": NG,
    "max2_rows": 32 * NG, "t2_ready": NP, "p2_out": NP, "pv2_step": NP,
    "o2_out": NG, "y_turned": NG, "inv2_out": NG, "y_out": NG, "y_stored": 16,
    **{f"stack2_{g}": 48 * FIRST_LOADS[g] for g in range(NG)},
    **{f"stack2_{g}_rest": 48 * (4 - FIRST_LOADS[g]) for g in range(NG)},
}
PER_BLOCK = {
    "xr_loaded": 16, "gate_ready": ITH, "up_ready": ITH, "silu_out": ITH, "inter_out": ITH,
    "inter_high": ITH, "inter_low": ITH, "down_done": ITH, "acc_out": ST, "stored": 16,
}


def attention_part(nc, psum, y_dram, x1_dram, x_lanes, x_rows, taps, conv_b, qkv_wT, qk_b, v_b, out_wT, out_b,
                   slopes, cond, w2T, att_b, aug_consts, pos):
    with ExitStack() as ctx:
        def sb(name, shape, dt=F32):
            return ctx.enter_context(nc.sbuf_tensor(name, shape, dt))

        def sem(name):
            return ctx.enter_context(nc.semaphore(name))

        S = {name: sem(name) for name in PER_BATCH}

        def at(b, name, count):
            return b * PER_BATCH[name] + count

        qkv_w = sb("qkv_w", [P, CT, 3 * D])
        out_w = sb("out_w", [P, CT, D])
        w2 = sb("w2", [P, 3, LT, L])
        tap = sb("tap", [P, CT, TAPS])
        conv_bias = sb("conv_bias", [P, CT])
        qk_bias = sb("qk_bias", [P, 8])
        v_bias = sb("v_bias", [P, D])
        out_bias = sb("out_bias", [P, D])
        slope = sb("slope", [H1, 1])
        aug_s = sb("aug_s", [2, 3])
        ident = sb("ident", [P, P])
        ident_b = sb("ident_b", [P, P], BF16)
        mask_q = sb("mask_q", [P, 2 * P], BF16)
        mask_k = sb("mask_k", [P, 2 * P], BF16)
        ones = sb("ones", [P, HD])

        h_in = sb("h_in", [P, CT, TAPS - 1 + L])
        h = sb("h", [P, CT, L])
        res = sb("res", [P, LT, D])
        high = sb("high", [P, 2048])
        low = sb("low", [P, 2048])
        alibi = high[0:H1, 0:4 * L].rearrange("h (i n) -> h i n", i=4)
        alibi_t = low[0:H1, 0:2 * L].rearrange("h (i n) -> h i n", i=2)
        pos_rows = low[0:H1, 2 * L:3 * L]
        one_rows = low[0:2, 1024:1024 + 512]
        q1 = sb("q1", [P, H1, L])
        k1 = sb("k1", [P, H1, L])
        v1 = sb("v1", [P, LT, D])
        max1 = sb("max1", [P, H1, LT])
        max1_h = sb("max1_h", [LT * H1, P])
        max1_l = sb("max1_l", [LT * H1, P])
        probs = sb("probs", [P, 2, GH, 512])
        inv1 = sb("inv1", [P, L])
        o1 = sb("o1", [P, CT, L])
        x1 = sb("x1", [P, LT, D])
        mask_row = sb("mask_row", [P, D])
        aug_f = sb("aug_f", [2, D])
        aug_h = sb("aug_h", [2, D])
        aug_l = sb("aug_l", [2, D])
        q2 = sb("q2", [P, SLOTS, GH, D])
        k2 = sb("k2", [P, SLOTS, GH, D])
        v2 = sb("v2", [P, CT, H2, 2 * DH])
        max2 = sb("max2", [P, NG, GH, CT])
        max2_h = sb("max2_h", [GH * CT, 2, P])
        max2_l = sb("max2_l", [GH * CT, 2, P])
        o2 = sb("o2", [P, D])
        inv2 = sb("inv2", [P, 2 * CT, 2, 1])
        y = sb("y", [P, CT, L])

        big_loaded = sem("big_loaded")
        qkv_loaded = sem("qkv_loaded")
        first_conv = sem("first_conv")
        small_loaded = sem("small_loaded")
        pads_zero = sem("pads_zero")
        zeroed = sem("zeroed")
        masks_made = sem("masks_made")
        ones_made = sem("ones_made")
        stacks_clear = sem("stacks_clear")
        alibi_step = sem("alibi_step")
        alibi_done = sem("alibi_done")
        fixed_rows = sem("fixed_rows")
        bias_scaled = sem("bias_scaled")
        N_BIG, N_SMALL, N_FIXED = 2, 10, 9

        block = ctx.enter_context(nc.Block())

        @block.sync
        def _(sp):
            def load_mask(src):
                sp.dma_start(mask_row[:], src.partition_broadcast(P)).then_inc(S["mask_loaded"], 16)
                for i in range(2):
                    sp.dma_start(aug_f[i:i + 1, :], src.partition_broadcast(1)).then_inc(S["mask_loaded"], 16)

            sp.wait_ge(pads_zero, 1)
            sp.dma_start(h_in[:, :, TAPS - 1:], x_lanes[B - 1]).then_inc(S["x_loaded"], 16)
            sp.dma_start(res[:], x_rows[B - 1]).then_inc(S["res_loaded"], 16)
            load_mask(cond[B - 1])

            for dst, src in ((tap[:], taps.rearrange("(c p) k -> p c k", p=P)), (conv_bias[:], conv_b),
                             (qk_bias[:], qk_b), (v_bias[:], v_b.partition_broadcast(P)),
                             (out_bias[:], out_b.partition_broadcast(P)), (slope[:], slopes),
                             (aug_s[:, 0:2], aug_consts[:, 0:2]), (aug_s[0:1, 2:3], att_b),
                             (aug_s[1:2, 2:3], aug_consts[1:2, 2:3]),
                             (pos_rows, pos.partition_broadcast(H1))):
                sp.dma_start(dst, src).then_inc(small_loaded, 16)
            sp.dma_start(qkv_w[:], qkv_wT.rearrange("(c p) n -> p c n", p=P)).then_inc(qkv_loaded, 16)
            sp.dma_start(out_w[:], out_wT.rearrange("(c p) n -> p c n", p=P)).then_inc(big_loaded, 16)
            sp.dma_start(w2[:].rearrange("p i c n -> p (i c) n"), w2T.rearrange("(m p) n -> p m n", p=P))\
                .then_inc(big_loaded, 16)
            sp.wait_ge(small_loaded, 16 * N_SMALL)
            sp.wait_ge(stacks_clear, 4)
            sp.wait_ge(alibi_done, 4)
            sp.wait_ge(ones_made, 2)
            for i in range(4):
                sp.dma_start(q1[ALIBI + i:ALIBI + i + 1, :, :], alibi[:, i, :]).then_inc(fixed_rows, 16)
            for i in range(2):
                sp.dma_start(k1[ALIBI + i:ALIBI + i + 1, :, :], pos_rows).then_inc(fixed_rows, 16)
            for stack, row in ((q2, DH), (q2, 2 * BLK + DH), (k2, MAX2)):
                sp.dma_start(stack[row:row + 2, :, :, :].rearrange("p s g n -> p (s g) n"),
                             one_rows[:, None, :].broadcast_to([2, SLOTS * GH, 512])).then_inc(fixed_rows, 16)

            def stacks1(b):
                for n, (stack, blocks) in enumerate(((q1, QUERY_BLOCKS), (k1, KEY_BLOCKS))):
                    sp.wait_ge(S["high1"], at(b, "high1", n + 1))
                    for e in range(4):
                        for r, is_low in blocks:
                            if e == 0 and is_low:
                                sp.wait_ge(S["low1"], at(b, "low1", n + 1))
                            part = low if is_low else high
                            sp.dma_start(
                                stack[r * HD:(r + 1) * HD, :, :].rearrange("p (o e) n -> p o e n", e=4)[:, :, e, :],
                                part[e * HD:(e + 1) * HD, n * 1024:(n + 1) * 1024].rearrange("p (o n) -> p o n", o=4)
                            ).then_inc(S[f"keys1_{e}" if n else "queries1"], 16)

            def batch(b, last):
                def wait(name, count):
                    sp.wait_ge(S[name], at(b, name, count))

                wait("pv1_ready", CT)
                if not last:
                    sp.dma_start(h_in[:, :, TAPS - 1:], x_lanes[b]).then_inc(S["x_loaded"], 16)
                wait("x1_out", LT)
                sp.dma_start(x1_dram[b], x1[:]).then_inc(S["x1_stored"], 16)
                wait("x1_stored", 16)
                if not last:
                    sp.dma_start(res[:], x_rows[b]).then_inc(S["res_loaded"], 16)
                wait("aug_low", 1)
                for r, part in ((0, aug_h), (2, aug_l)):
                    sp.dma_start(k2[r * BLK + DH:r * BLK + DH + 2, :, :, :].rearrange("p s g n -> p (s g) n"),
                                 part[:, None, :].broadcast_to([2, SLOTS * GH, D])).then_inc(S["aug_rows"], 16)
                for g in range(NG):
                    if g >= SLOTS:
                        wait("t2_ready", 2 * CT * (g - SLOTS + 1))
                    order = (("q", 0), ("q", 1), ("k", 0), ("k", 1)) if g == 0 else \
                        (("q", 0), ("k", 0), ("q", 1), ("k", 1))
                    for step, (which, e) in enumerate(order):
                        off, stack, blocks = (0, q2, QUERY_BLOCKS) if which == "q" else (1024, k2, KEY_BLOCKS)
                        if g == 0:
                            wait("high2", 1 + off // 1024)
                        loaded = f"stack2_{g}" if step < FIRST_LOADS[g] else f"stack2_{g}_rest"
                        row = (2 * g + e) * DH
                        for r, is_low in blocks:
                            if g == 0 and is_low:
                                wait("low2", 1 + off // 1024)
                            part = low if is_low else high
                            sp.dma_start(
                                stack[r * BLK:r * BLK + DH, g % SLOTS, :, :]
                                .rearrange("p (t e) n -> p t e n", e=2)[:, :, e, :],
                                part[row:row + DH, off:off + 1024].rearrange("p (t n) -> p t n", t=2)
                            ).then_inc(S[loaded], 16)
                if not last:
                    stacks1(b + 1)
                wait("y_out", NG)
                sp.dma_start(y_dram[b], y[:]).then_inc(S["y_stored"], 16)
                wait("y_stored", 16)
                if not last:
                    load_mask(cond[b])

            stacks1(0)
            with sp.Fori(0, B - 1) as b:
                batch(b, last=False)
            batch(B - 1, last=True)

        @block.gpsimd
        def _(pool):
            pool.memset(h_in[:], 0.0).then_inc(pads_zero, 1)
            pool.memset(ident[:], 0.0).then_inc(zeroed, 1)
            pool.memset(ident_b[:], 0.0).then_inc(zeroed, 1)
            pool.memset(mask_q[:, 0:P], 0.0).then_inc(zeroed, 1)
            pool.memset(mask_k[:, P:2 * P], 0.0).then_inc(zeroed, 1)
            pool.memset(mask_q[:, P:2 * P], NEG1).then_inc(masks_made, 1)
            pool.memset(mask_k[:, 0:P], NEG1).then_inc(masks_made, 1)
            pool.wait_ge(zeroed, 4)
            for t in (ident, ident_b):
                pool.affine_select(out=t[:], in_=t[:], compare_op=ALU.not_equal, fill=1.0, base=0,
                                   pattern=[[-1, P]], channel_multiplier=1).then_inc(masks_made, 1)
            pool.affine_select(out=mask_q[:, 0:P], in_=mask_q[:, 0:P], compare_op=ALU.is_ge, fill=NEG1, base=0,
                               pattern=[[-1, P]], channel_multiplier=1).then_inc(masks_made, 1)
            pool.affine_select(out=mask_k[:, P:2 * P], in_=mask_k[:, P:2 * P], compare_op=ALU.is_ge, fill=NEG1,
                               base=0, pattern=[[1, P]], channel_multiplier=-1).then_inc(masks_made, 1)
            pool.wait_ge(masks_made, 6)
            for t in (q1, k1):
                pool.memset(t[ALIBI:P, :, :], 1.0).then_inc(stacks_clear, 1)
            pool.wait_ge(stacks_clear, 2)
            for t in (q2, k2):
                pool.memset(t[:], 0.0).then_inc(stacks_clear, 1)
            pool.wait_ge(stacks_clear, 4)
            pool.wait_ge(small_loaded, 16 * N_SMALL)

            def residual_and_mask(res_loaded, mask_loaded, aug_steps):
                pool.wait_ge(S["res_loaded"], res_loaded)
                nc.gpsimd.tensor_tensor(res[:], res[:], out_bias[:, None, :].broadcast_to([P, LT, D]), ALU.add)\
                    .then_inc(S["res_biased"], 1)
                pool.wait_ge(S["mask_loaded"], mask_loaded)
                for i, op in enumerate((ALU.mult, ALU.add, ALU.mult)):
                    if i:
                        pool.wait_ge(S["aug_step"], aug_steps + i)
                    nc.gpsimd.tensor_tensor(aug_f[:], aug_f[:], aug_s[:, i:i + 1].broadcast_to([2, D]), op)\
                        .then_inc(S["aug_step"], 1)

            residual_and_mask(16, 48, 0)
            with pool.Fori(0, B - 1) as b:
                def wait(name, count):
                    pool.wait_ge(S[name], at(b, name, count))

                wait("x_loaded", PER_BATCH["x_loaded"] + 16)
                products = v1[:].rearrange("p t (u n) -> p (t u) n", n=L)

                def over(t):
                    return t.broadcast_to([P, CT, L])

                nc.gpsimd.tensor_tensor(h[:], h_in[:, :, 0:L], over(tap[:, :, 0:1]), ALU.mult)\
                    .then_inc(S["conv_step"], 1)
                wait("conv_step", 1)
                nc.gpsimd.tensor_tensor(h[:], h[:], over(conv_bias[:, :, None]), ALU.add).then_inc(S["conv_step"], 1)
                for k in range(1, TAPS):
                    if k > 1:
                        wait("conv_step", 2 * k)
                    nc.gpsimd.tensor_tensor(products, h_in[:, :, k:k + L], over(tap[:, :, k:k + 1]), ALU.mult)\
                        .then_inc(S["conv_step"], 1)
                    wait("conv_step", 2 * k + 1)
                    nc.gpsimd.tensor_tensor(h[:], h[:], products, ALU.add).then_inc(S["conv_step"], 1)
                residual_and_mask(at(b, "res_loaded", 32), at(b, "mask_loaded", 96), at(b, "aug_step", 3))

        @block.scalar
        def _(act):
            act.wait_ge(small_loaded, 16 * N_SMALL)
            act.wait_ge(bias_scaled, 1)
            act.wait_ge(fixed_rows, 16 * N_FIXED)

            def queries_keys1(b, o):
                act.wait_ge(S["qk1_ready"], at(b, "qk1_ready", o + 1))
                nc.scalar.activation(low[:, o * L:(o + 1) * L], psum[:, o % 2, 0:L], ACT.Identity,
                                     bias=qk_bias[:, o:o + 1], scale=SCALE1 if o < 4 else 1.0)\
                    .then_inc(S["qk1_out"], 1)

            def batch(b, last):
                def wait(name, count):
                    act.wait_ge(S[name], at(b, name, count))

                wait("max1_high", 1)
                wait("max1_low", 1)
                for i, part in enumerate((max1_h, max1_l)):
                    act.dma_start(q1[MAX1 + i:MAX1 + i + 1, :, :].rearrange("p h (t n) -> p (h t) n", t=LT),
                                  part[:, :]).then_inc(S["max1_rows"], 16)
                for p in range(H1 // 2):
                    g = p // 2
                    wait("t1_ready", p + 1)
                    if g >= 2:
                        wait("pv1_ready", g - 1)
                    nc.scalar.activation(probs[:, g % 2, p % 2 * 2:p % 2 * 2 + 2, :],
                                         psum[:, 2 + p % 2 * 2:4 + p % 2 * 2, :], ACT.Exp).then_inc(S["p1_out"], 1)
                wait("t1_ready", H1 // 2)
                for t in range(LT):
                    wait("q2_ready", t + 1)
                    nc.scalar.activation(low[:, t * D:(t + 1) * D], psum[:, 2 + t, :], ACT.Identity, scale=SCALE2)\
                        .then_inc(S["q2_out"], 1)

                def max_rows(g):
                    wait("max2_high", g + 1)
                    wait("max2_low", g + 1)
                    for i, part in enumerate((max2_h, max2_l)):
                        act.dma_start(q2[MAX2 + i:MAX2 + i + 1, g % SLOTS, :, :]
                                      .rearrange("p h (t n) -> p (h t) n", t=CT), part[:, g % 2, :])\
                            .then_inc(S["max2_rows"], 16)

                def o2_evac(g):
                    wait("pv2_step", 2 * CT * (g + 1))
                    if g:
                        wait("y_turned", g)
                    nc.scalar.activation(o2[:], psum[:, 6, :], ACT.Copy).then_inc(S["o2_out"], 1)

                wait("pv1_ready", CT)
                max_rows(0)
                for n in range(FOLLOW, N_STEPS):
                    j = (n - FOLLOW) // 2
                    if (n - FOLLOW) % 2 == 0 and j < NP:
                        g, u = j // (2 * CT), j % (2 * CT)
                        wait("t2_ready", j + 1)
                        if j >= 4:
                            wait("pv2_step", j - 2 - j % 2)
                        nc.scalar.activation(probs[:, u // 2 % 2, u % 2 * 2:u % 2 * 2 + 2, :],
                                             psum[:, 2 + u % 2 * 2:4 + u % 2 * 2, :], ACT.Exp)\
                            .then_inc(S["p2_out"], 1)
                        if u == LAG - 1 and g >= 1:
                            o2_evac(g - 1)
                        if u == 5 and g + 1 < NG:
                            max_rows(g + 1)
                    if n in QK1_AT and not last:
                        queries_keys1(b + 1, QK1_AT.index(n))
                o2_evac(NG - 1)

            for o in range(8):
                queries_keys1(0, o)
            with act.Fori(0, B - 1) as b:
                batch(b, last=False)
            batch(B - 1, last=True)

        @block.vector
        def _(dve):
            nc.vector.memset(ones[:], 1.0).then_inc(ones_made, 1)
            nc.vector.memset(one_rows, 1.0).then_inc(ones_made, 1)
            nc.vector.memset(v2[:], 1.0).then_inc(ones_made, 1)
            dve.wait_ge(small_loaded, 16 * N_SMALL)
            nc.vector.tensor_scalar(alibi_t[:, 0, :], pos_rows, 0.0, slope[:, 0:1], ALU.mult, ALU.add)\
                .then_inc(alibi_step, 1)
            nc.vector.tensor_scalar(alibi_t[:, 1, :], pos_rows, slope[:, 0:1], -1.0, ALU.mult, ALU.mult)\
                .then_inc(alibi_step, 1)
            nc.vector.tensor_scalar(qk_bias[:, 0:4], qk_bias[:, 0:4], SCALE1, None, ALU.mult).then_inc(bias_scaled, 1)
            dve.wait_ge(alibi_step, 2)
            for i in range(2):
                nc.vector.tensor_copy(alibi[:, 2 * i, :].bitcast(F32R), alibi_t[:, i, :]).then_inc(alibi_done, 1)
            dve.wait_ge(alibi_done, 2)
            for i in range(2):
                nc.vector.tensor_tensor(alibi[:, 2 * i + 1, :], alibi_t[:, i, :], alibi[:, 2 * i, :], ALU.subtract)\
                    .then_inc(alibi_done, 1)
            dve.wait_ge(S["x_loaded"], 16)
            for c in range(CT):
                nc.vector.tensor_scalar(h[:, c, :], h_in[:, c, 0:L], tap[:, c, 0:1], conv_bias[:, c:c + 1],
                                        ALU.mult, ALU.add).then_inc(first_conv, 1)
            for k in range(1, TAPS):
                for c in range(CT):
                    dve.wait_ge(first_conv, CT * (k - 1) + c + 1)
                    nc.vector.scalar_tensor_tensor(out=h[:, c, :], in0=h_in[:, c, k:k + L], scalar=tap[:, c, k:k + 1],
                                                   in1=h[:, c, :], op0=ALU.mult, op1=ALU.add).then_inc(first_conv, 1)
            dve.wait_ge(ones_made, 3)
            dve.wait_ge(fixed_rows, 16 * N_FIXED)

            def split(b, half, high_sem, low_sem):
                cols = slice(half * 1024, (half + 1) * 1024)
                nc.vector.tensor_copy(high[:, cols].bitcast(F32R), low[:, cols]).then_inc(S[high_sem], 1)
                dve.wait_ge(S[high_sem], at(b, high_sem, half + 1))
                nc.vector.tensor_tensor(low[:, cols], low[:, cols], high[:, cols], ALU.subtract)\
                    .then_inc(S[low_sem], 1)

            def split1(b, half):
                dve.wait_ge(S["qk1_out"], at(b, "qk1_out", 4 * half + 4))
                split(b, half, "high1", "low1")

            def values1(b, t):
                dve.wait_ge(S["v1_ready"], at(b, "v1_ready", t + 1))
                nc.vector.tensor_tensor(v1[:, t, :], psum[:, V1_BANKS[t], :], v_bias[:], ALU.add)\
                    .then_inc(S["v1_out"], 1)

            def batch(b, last):
                def wait(name, count):
                    dve.wait_ge(S[name], at(b, name, count))

                for n in range(0, H1, 2):
                    wait("s1_ready", n // 2 + 1)
                    i, bank = n % 4 * 4 + n // 4, S1_BANKS[n // 2 % 2]
                    for t in range(LT):
                        last_max = nc.vector.reduce_max(max1[:, i:i + 5:4, t],
                                                        psum[:, bank:bank + 2, t * L:t * L + (t + 1) * P], AX_X)
                    last_max.then_inc(S["s1_max"], 1)
                wait("max1_turned", 1)
                turned = psum[0:LT * H1, 7, 0:P]
                nc.vector.tensor_scalar(max1_h[:].bitcast(F32R), turned, -1.0, None, ALU.mult)\
                    .then_inc(S["max1_high"], 1)
                wait("max1_high", 1)
                nc.vector.scalar_tensor_tensor(out=max1_l[:], in0=turned, scalar=-1.0, in1=max1_h[:],
                                               op0=ALU.mult, op1=ALU.subtract).then_inc(S["max1_low"], 1)
                values1(b, 1)
                for g in range(CT):
                    wait("pv1_ready", g + 1)
                    if g:
                        wait("o1_out", g)
                    nc.vector.reciprocal(inv1[:], psum[:, 6 + g % 2, L:2 * L]).then_inc(S["inv1_out"], 1)
                    wait("inv1_out", g + 1)
                    nc.vector.tensor_tensor(o1[:, g, :], psum[:, 6 + g % 2, 0:L], inv1[:], ALU.mult)\
                        .then_inc(S["o1_out"], 1)
                wait("res_biased", 1)
                for t in range(LT):
                    wait("proj_ready", t + 1)
                    nc.vector.tensor_tensor(x1[:, t, :], psum[:, t, :], res[:, t, :], ALU.add)\
                        .then_inc(S["x1_out"], 1)
                wait("aug_step", 3)
                nc.vector.tensor_copy(aug_h[:].bitcast(F32R), aug_f[:]).then_inc(S["aug_high"], 1)
                wait("aug_high", 1)
                nc.vector.tensor_tensor(aug_l[:], aug_f[:], aug_h[:], ALU.subtract).then_inc(S["aug_low"], 1)
                wait("mask_loaded", 48)
                wait("q2_out", LT)
                split(b, 0, "high2", "low2")
                for t in range(LT):
                    wait("k2_ready", t + 1)
                    nc.vector.tensor_tensor(low[:, (2 + t) * D:(3 + t) * D], psum[:, 4 + t, :], mask_row[:], ALU.mult)\
                        .then_inc(S["k2_out"], 1)
                wait("k2_out", LT)
                split(b, 1, "high2", "low2")
                for t in range(CT):
                    wait("v2_ready", t + 1)
                    nc.vector.tensor_copy(v2[:, t, :, 0:DH],
                                          psum[:, V2_BANKS[t], 0:L].rearrange("p (h d) -> p h d", h=H2))\
                        .then_inc(S["v2_out"], 1)

                def maximum(n):
                    wait("s2_ready", n + 1)
                    g, e, t = n // GS, HEAD_ORDER[n % GS // CT], n % CT
                    nc.vector.reduce_max(max2[:, g, e, t:t + 1], psum[:, n % 2, :], AX_X).then_inc(S["s2_max"], 1)

                def turn(g):
                    wait("max2_turned", g + 1)
                    if g >= 2:
                        wait("max2_rows", 32 * (g - 1))
                    rows = psum[0:GH * CT, 7, 0:P]
                    nc.vector.tensor_scalar(max2_h[:, g % 2, :].bitcast(F32R), rows, -1.0, None, ALU.mult)\
                        .then_inc(S["max2_high"], 1)
                    wait("max2_high", g + 1)
                    nc.vector.scalar_tensor_tensor(out=max2_l[:, g % 2, :], in0=rows, scalar=-1.0,
                                                   in1=max2_h[:, g % 2, :], op0=ALU.mult, op1=ALU.subtract)\
                        .then_inc(S["max2_low"], 1)

                def outputs(g):
                    wait("y_turned", g + 1)
                    if g:
                        wait("y_out", g)
                    heads = psum[:, 7, :].rearrange("p (q e d) -> p q e d", e=2, d=2 * DH)
                    nc.vector.reciprocal(inv2[:], heads[:, :, :, DH:DH + 1]).then_inc(S["inv2_out"], 1)
                    wait("inv2_out", g + 1)
                    dst = y[:].rearrange("p c (t x d) -> p (c t) x d", t=2, d=DH)[:, :, 2 * g:2 * g + 2, :]
                    nc.vector.tensor_tensor(dst, heads[:, :, :, 0:DH],
                                            inv2[:].broadcast_to([P, 2 * CT, 2, DH]), ALU.mult)\
                        .then_inc(S["y_out"], 1)

                for n in range(N_STEPS):
                    if n < NS:
                        maximum(n)
                    if n >= TURN_AT and (n - TURN_AT) % GS == 0 and n < NS:
                        turn((n - TURN_AT) // GS)
                    if n == NS:
                        turn(NG - 1)
                    if n >= OUT_AT and (n - OUT_AT) % GS == 0:
                        outputs((n - OUT_AT) // GS)
                    for half in range(2):
                        if n == QK1_AT[4 * half + 3] + 1 and not last:
                            split1(b + 1, half)
                outputs(NG - 1)
                if not last:
                    values1(b + 1, 0)

            for half in range(2):
                split1(0, half)
            values1(0, 0)
            with dve.Fori(0, B - 1) as b:
                batch(b, last=False)
            batch(B - 1, last=True)

        @block.tensor
        def _(pe):
            pe.wait_ge(qkv_loaded, 16)
            pe.wait_ge(masks_made, 6)
            pe.wait_ge(ones_made, 3)

            def r(ap):
                return ap.bitcast(F32R)

            def queries_keys1(b, o):
                if o >= 2:
                    pe.wait_ge(S["qk1_out"], at(b, "qk1_out", o - 1))
                for c in range(CT):
                    last = nc.tensor.matmul(psum[:, o % 2, 0:L], qkv_w[:, c, o * P:(o + 1) * P], h[:, c, :],
                                            start=c == 0, stop=c == CT - 1)
                last.then_inc(S["qk1_ready"], 1)

            def values(t):
                for c in range(CT):
                    last = nc.tensor.matmul(psum[:, V1_BANKS[t], :], h[:, c, t * P:(t + 1) * P],
                                            qkv_w[:, c, 2 * D:3 * D], start=c == 0, stop=c == CT - 1)
                last.then_inc(S["v1_ready"], 1)

            def batch(b, last_batch):
                def wait(name, count):
                    pe.wait_ge(S[name], at(b, name, count))

                pe.wait_ge(fixed_rows, 16 * N_FIXED)
                wait("queries1", 12 * 16)
                wait("qk1_out", 8)
                for n in range(H1):
                    i = n % 4 * 4 + n // 4
                    if n % 4 == 0:
                        wait(f"keys1_{n // 4}", 48)
                    if n >= 4 and n % 2 == 0:
                        wait("s1_max", n // 2 - 1)
                    bank = psum[:, S1_BANKS[n // 2 % 2] + n % 2, :]
                    for t in range(LT):
                        nc.tensor.matmul(bank[:, t * L:(t + 1) * L], r(q1[0:MAX1, i, t * P:(t + 1) * P]),
                                         r(k1[0:MAX1, i, :]), start=t == 0, stop=False, skip_group_check=True)
                    nc.tensor.matmul(bank[:, 0:L], ident_b[:], mask_q[:], start=False, stop=False,
                                     skip_group_check=True)
                    last = nc.tensor.matmul(bank[:, L + P:2 * L], ident_b[:], mask_q[:, 0:P], start=False, stop=True,
                                            skip_group_check=True)
                    if n % 2:
                        last.then_inc(S["s1_ready"], 1)
                wait("s1_max", H1 // 2)
                nc.tensor.transpose(psum[0:LT * H1, 7, 0:P], max1[:].rearrange("p h t -> p (h t)"), ident[:])\
                    .then_inc(S["max1_turned"], 1)

                def values1(g):
                    wait("p1_out", 2 * g + 2)
                    if g == 1:
                        wait("max1_low", 1)
                    elif g >= 2:
                        wait("o1_out", g - 1)
                    for stat, col in ((v1, 0), (None, L)):
                        for kt in range(LT):
                            for e in range(4):
                                lhsT = v1[:, kt, (4 * g + e) * HD:(4 * g + e + 1) * HD] if stat is v1 else ones[:]
                                last = nc.tensor.matmul(
                                    psum[e * HD:(e + 1) * HD, 6 + g % 2, col + kt * P:col + L], lhsT,
                                    probs[:, g % 2, e, kt * L + kt * P:(kt + 1) * L],
                                    start=kt == 0, stop=kt == LT - 1, skip_group_check=True)
                    last.then_inc(S["pv1_ready"], 1)

                values(1)
                wait("v1_out", LT)
                wait("max1_rows", 32)
                for p in range(H1 // 2):
                    if p >= 2:
                        wait("p1_out", p - 1)
                    for e in range(2):
                        i = 2 * p + e
                        bank = psum[:, 2 + p % 2 * 2 + e, :]
                        for t in range(LT):
                            nc.tensor.matmul(bank[:, t * L:(t + 1) * L], r(k1[0:END1, i, t * P:(t + 1) * P]),
                                             r(q1[0:END1, i, :]), start=t == 0, stop=False, skip_group_check=True)
                        nc.tensor.matmul(bank[:, 0:P], ident_b[:], mask_k[:, P:2 * P], start=False, stop=False,
                                         skip_group_check=True)
                        last = nc.tensor.matmul(bank[:, L:2 * L], ident_b[:], mask_k[:], start=False, stop=True,
                                                skip_group_check=True)
                    last.then_inc(S["t1_ready"], 1)
                    if p % 2 == 1 and p >= 3:
                        values1(p // 2 - 1)
                values1(CT - 1)
                wait("s1_max", H1 // 2)
                for t in range(LT):
                    for c in range(CT):
                        if t == 0:
                            wait("o1_out", c + 1)
                        last = nc.tensor.matmul(psum[:, t, :], o1[:, c, t * P:(t + 1) * P], out_w[:, c, :],
                                                start=c == 0, stop=c == CT - 1)
                    last.then_inc(S["proj_ready"], 1)
                wait("x1_out", LT)
                wait("p1_out", H1 // 2)
                for i, ready in ((0, "q2_ready"), (1, "k2_ready")):
                    for o in range(LT):
                        for t in range(LT):
                            last = nc.tensor.matmul(psum[:, 2 + 2 * i + o, :], w2[:, i, t, o * P:(o + 1) * P],
                                                    x1[:, t, :], start=t == 0, stop=t == LT - 1)
                        last.then_inc(S[ready], 1)
                for n in range(CT):
                    for t in range(LT):
                        last = nc.tensor.matmul(psum[:, V2_BANKS[n], 0:L],
                                                x1[:, t, n * P:(n + 1) * P], w2[:, 2, t, :],
                                                start=t == 0, stop=t == LT - 1, skip_group_check=True)
                    last.then_inc(S["v2_ready"], 1)

                def scores(s):
                    g, n = s // GS, s % GS
                    if n == 0:
                        wait(f"stack2_{g}", 48 * FIRST_LOADS[g])
                        if g == 0:
                            wait("aug_rows", 32)
                    if n == GS // 2:
                        wait(f"stack2_{g}_rest", 48 * (4 - FIRST_LOADS[g]))
                    if s < 2:
                        wait("v2_out", CT)
                    else:
                        wait("s2_max", s - 1)
                    slot, e, t = g % SLOTS, HEAD_ORDER[n // CT], n % CT
                    nc.tensor.matmul(psum[:, s % 2, :], r(q2[0:MAX2, slot, e, t * P:(t + 1) * P]),
                                     r(k2[0:MAX2, slot, e, :]), start=True, stop=True).then_inc(S["s2_ready"], 1)

                def turn(g):
                    wait("s2_max", GH * CT * (g + 1))
                    if g == 0:
                        wait("o1_out", CT)
                    elif g == NG - 1:
                        wait("y_out", 1)
                    nc.tensor.transpose(psum[0:GH * CT, 7, 0:P], max2[:, g].rearrange("p h t -> p (h t)"), ident[:])\
                        .then_inc(S["max2_turned"], 1)

                def shifted(j):
                    g, u = j // (2 * CT), j % (2 * CT)
                    if u == 0:
                        wait("max2_rows", 32 * (g + 1))
                    if j < 2:
                        wait("q2_out", LT)
                        wait("k2_out", LT)
                    else:
                        wait("p2_out", j - 1)
                    kt, slot = u // 2, g % SLOTS
                    for e in range(2):
                        i = u % 2 * 2 + e
                        last = nc.tensor.matmul(psum[:, 2 + i, :], r(k2[0:END2, slot, i, kt * P:(kt + 1) * P]),
                                                r(q2[0:END2, slot, i, :]), start=True, stop=True)
                    last.then_inc(S["t2_ready"], 1)

                def values2(j):
                    g, kt, half = j // (2 * CT), j % (2 * CT) // 2, j % 2
                    wait("p2_out", j + 2 - half)
                    queries = slice(half * D // 2, (half + 1) * D // 2)
                    if half == 0 and kt == 0:
                        if g == 0:
                            wait("o1_out", CT)
                        else:
                            wait("o2_out", g)
                    for e in range(GH):
                        head = (e // 2) * 8 + 2 * g + e % 2
                        last = nc.tensor.matmul(psum[e * BLK:(e + 1) * BLK, 6, queries], v2[:, kt, head, :],
                                                probs[:, kt % 2, e, queries], start=kt + half == 0, stop=kt == CT - 1,
                                                skip_group_check=True)
                    last.then_inc(S["pv2_step"], 1)

                def turn_outputs(g):
                    wait("o2_out", g + 1)
                    if g < 2:
                        wait("max2_low", g + 3)
                    else:
                        wait("y_out", g)
                    for t in range(CT):
                        last = nc.tensor.transpose(psum[:, 7, t * P:(t + 1) * P], o2[:, t * P:(t + 1) * P], ident[:])
                    last.then_inc(S["y_turned"], 1)

                for n in range(N_STEPS):
                    if n < NS:
                        scores(n)
                    if n >= TURN_AT and (n - TURN_AT) % GS == 0 and n < NS:
                        turn((n - TURN_AT) // GS)
                    if n == NS:
                        turn(NG - 1)
                    j = (n - FOLLOW) // 2
                    if n >= FOLLOW and (n - FOLLOW) % 2 == 0 and j < NP:
                        shifted(j)
                    if n >= FOLLOW and (n - FOLLOW) % 2 == 1 and j >= LAG:
                        values2(j - LAG)
                    if n >= OUT_AT and (n - OUT_AT) % GS == 0:
                        turn_outputs((n - OUT_AT) // GS)
                    if n in QK1_AT and not last_batch:
                        if n == QK1_AT[0]:
                            wait("s2_max", NS)
                            wait("conv_step", CONV_STEPS)
                        queries_keys1(b + 1, QK1_AT.index(n))
                turn_outputs(NG - 1)
                if not last_batch:
                    values(0)

            pe.wait_ge(first_conv, TAPS * CT)
            for o in range(8):
                queries_keys1(0, o)
            values(0)
            pe.wait_ge(big_loaded, 16 * N_BIG)
            with pe.Fori(0, B - 1) as b:
                batch(b, last_batch=False)
            batch(B - 1, last_batch=True)


def feed_forward_part(nc, psum, y_dram, x1_dram, ctrl, spline_m, spline_r, seg_mask, out):
    with ExitStack() as ctx:
        def sb(name, shape, dt=F32):
            return ctx.enter_context(nc.sbuf_tensor(name, shape, dt))

        def sem(name):
            return ctx.enter_context(nc.semaphore(name))

        S = {name: sem(name) for name in PER_BLOCK}

        def at(half, b, name, count):
            return (b + half * NTB) * PER_BLOCK[name] + count

        def r(ap):
            return ap.bitcast(F32R)

        x1_blocks = x1_dram.rearrange("(n k) p t d -> n p k t d", n=NTB)
        out_blocks = out.rearrange("(n k) p t d -> n p k t d", n=NTB)
        w_h = [sb(f"w_{n}_h", [P, HALF]) for n in ("gate", "up", "down")]
        w_l = [sb(f"w_{n}_l", [P, HALF]) for n in ("gate", "up", "down")]
        y_h = sb("y_all_h", [P, CT, B * L])
        y_l = sb("y_all_l", [P, CT, B * L])
        stage = sb("stage", [P, ST, TB])
        points = stage[0:NW * 32, 0:2, :]
        products = stage[0:NW * 32, 2:4, :]
        x_res = stage
        x_res_batches = x_res[:].rearrange("p (k t) d -> p k t d", t=LT)
        powers_h = sb("powers_h", [NW * 32, 2 * NW, P])
        powers_l = sb("powers_l", [NW * 32, 2 * NW, P])
        points_h = sb("points_h", [NW * 32, 2, 512])
        points_l = sb("points_l", [NW * 32, 2, 512])
        seg_words = sb("seg", [P, 2, HALF // 4], I32)
        seg = seg_words[:].rearrange("p o n -> p (o n)").bitcast(U8).rearrange("p (o n) -> p o n", o=2)
        scratch = sb("scratch", [P, 4, 512])
        powers = scratch[0:NW * 32, 0:2, :].rearrange("p s n -> p (s n)")[:, 0:2 * NW * P]
        weights = scratch
        silu = scratch[:, 0, :]
        inter = scratch[:, 1, :]
        inter_h = sb("inter_h", [P, 2, TB])
        inter_l = sb("inter_l", [P, 2, TB])

        y_loaded = [sem(f"y_loaded{i}") for i in range(2)]
        y_high = sem("y_high")
        y_low = sem("y_low")
        tables_loaded = sem("tables_loaded")
        seg_loaded = sem("seg_loaded")
        powers_high = sem("powers_high")
        powers_low = sem("powers_low")
        points_loaded = [sem(f"points_loaded{i}") for i in range(2)]
        points_scaled = sem("points_scaled")
        points_high = sem("points_high")
        points_low = sem("points_low")
        segs_ready = sem("segs_ready")
        first_out = sem("first_out")
        second_out = sem("second_out")
        weights_high = sem("weights_high")
        weights_low = sem("weights_low")

        block = ctx.enter_context(nc.Block())

        def units(half):
            return range(half * NW * NUH, (half + 1) * NW * NUH)

        def cols(n):
            u = n // NW % NUH
            return slice(u * 512, (u + 1) * 512)

        @block.sync
        def _(sp):
            def load_points(u):
                k = u % 2
                if u >= 2:
                    sp.wait_ge(points_low, u - 1)
                sp.dma_start(points[:, k, :], ctrl[:, u * 512:(u + 1) * 512]).then_inc(points_loaded[k], 16)
                sp.dma_start(products[:, k, :], spline_m[:, u * 512:(u + 1) * 512]).then_inc(points_loaded[k], 16)

            sp.dma_start(powers, spline_r).then_inc(tables_loaded, 16)
            load_points(0)
            sp.dma_start(seg_words[:], seg_mask[:, 0]).then_inc(seg_loaded, 16)
            for u in range(1, NUH + 2):
                load_points(u)
                if u <= 2:
                    for i in range((u - 1) * B // 2, u * B // 2):
                        sp.dma_start(y_l[:, :, i * L:(i + 1) * L], y_dram[i]).then_inc(y_loaded[u - 1], 16)
            sp.wait_ge(second_out, NW * NUH)
            sp.dma_start(seg_words[:], seg_mask[:, 1]).then_inc(seg_loaded, 16)
            for half, dst in enumerate((x1_blocks, out_blocks)):
                if half:
                    for u in range(NUH + 2, 2 * NUH):
                        load_points(u)
                sp.wait_ge(points_low, 2 * NUH if half else NUH + 2)

                def load(b):
                    sp.dma_start(x_res_batches, x1_blocks[b]).then_inc(S["xr_loaded"], 16)

                def store(b):
                    sp.wait_ge(S["acc_out"], at(half, b, "acc_out", ST))
                    sp.dma_start(dst[b], x_res_batches).then_inc(S["stored"], 16)
                    sp.wait_ge(S["stored"], at(half, b, "stored", 16))

                load(0)
                with sp.Fori(0, NTB - 1) as b:
                    store(b)
                    load(b + 1)
                store(NTB - 1)

        @block.gpsimd
        def _(pool):
            for u in range(2 * NUH):
                k = u % 2
                pool.wait_ge(points_loaded[k], 32 * (u // 2 + 1))
                nc.gpsimd.tensor_tensor(products[:, k, :], points[:, k, :], products[:, k, :], ALU.mult)\
                    .then_inc(points_scaled, 1)
                pool.wait_ge(points_high, u + 1)
                nc.gpsimd.tensor_tensor(r(points_l[:, k, :]), products[:, k, :], points_h[:, k, :], ALU.subtract)\
                    .then_inc(points_low, 1)

        @block.tensor
        def _(pe):
            for half in range(2):
                if half:
                    pe.wait_ge(S["acc_out"], NTB * ST)
                else:
                    pe.wait_ge(powers_low, 1)
                for n in units(half):
                    i, k = n % NW, n // NW % 2
                    if i == 0:
                        pe.wait_ge(points_low, n // NW + 1)
                    if n >= 4:
                        pe.wait_ge(second_out, n - 3)
                    for e in range(2):
                        bank = psum[:, 2 * (n % 4) + e, :]
                        nc.tensor.matmul(bank, r(powers_h[:, 2 * i + e, :]), r(points_h[:, k, :]), start=True, stop=False)
                        nc.tensor.matmul(bank, r(powers_h[:, 2 * i + e, :]), r(points_l[:, k, :]), start=False, stop=False)
                        last = nc.tensor.matmul(bank, r(powers_l[:, 2 * i + e, :]), r(points_h[:, k, :]),
                                                start=False, stop=True)
                    last.then_inc(segs_ready, 1)
                if half == 0:
                    pe.wait_ge(y_low, B)
                pe.wait_ge(second_out, NW * NUH * (half + 1))
                pe.wait_ge(weights_low, NW * NUH * (half + 1))

                with pe.Fori(0, NTB) as b:
                    def wait(name, count):
                        pe.wait_ge(S[name], at(half, b, name, count))

                    def gate_up(it):
                        if it >= 2:
                            wait("inter_out", it - 1)
                        for i, ready in ((0, "gate_ready"), (1, "up_ready")):
                            bank = psum[:, 4 + 2 * (it % 2) + i, :]
                            for c in range(CT):
                                lhs = slice((c * ITH + it) * P, (c * ITH + it + 1) * P)
                                rhs = (slice(None), c, bass.ts(b, TB))
                                nc.tensor.matmul(bank, r(w_h[i][:, lhs]), r(y_h[rhs]), start=c == 0, stop=False)
                                nc.tensor.matmul(bank, r(w_h[i][:, lhs]), r(y_l[rhs]), start=False, stop=False)
                                last = nc.tensor.matmul(bank, r(w_l[i][:, lhs]), r(y_h[rhs]),
                                                        start=False, stop=c == CT - 1)
                            last.then_inc(S[ready], 1)

                    def down(it):
                        wait("inter_low", it + 1)
                        rhs = slice(it * HIDDEN, (it + 1) * HIDDEN)
                        for s in range(ST):
                            lhs = (slice(None), it % 2, slice(s * P, (s + 1) * P))
                            nc.tensor.matmul(psum[:, s, :], r(inter_h[lhs]), r(w_h[2][:, rhs]),
                                             start=it == 0, stop=False)
                            nc.tensor.matmul(psum[:, s, :], r(inter_h[lhs]), r(w_l[2][:, rhs]), start=False, stop=False)
                            last = nc.tensor.matmul(psum[:, s, :], r(inter_l[lhs]), r(w_h[2][:, rhs]),
                                                    start=False, stop=it == ITH - 1)
                        last.then_inc(S["down_done"], 1)

                    gate_up(0)
                    for it in range(1, ITH):
                        gate_up(it)
                        down(it - 1)
                    down(ITH - 1)

        @block.scalar
        def _(act):
            def high_points(u):
                act.wait_ge(points_scaled, u + 1)
                if u >= 2:
                    act.wait_ge(segs_ready, NW * (u - 1))
                nc.scalar.activation(r(points_h[:, u % 2, :]), products[:, u % 2, :], ACT.Copy)\
                    .then_inc(points_high, 1)

            def high_weights(n):
                act.wait_ge(second_out, n + 1)
                nc.scalar.activation(r(w_h[n % NW][:, cols(n)]), weights[:, n % 4, :], ACT.Copy)\
                    .then_inc(weights_high, 1)

            act.wait_ge(tables_loaded, 16)
            nc.scalar.activation(r(powers_h[:].rearrange("p a n -> p (a n)")), powers, ACT.Copy)\
                .then_inc(powers_high, 1)
            high_points(0)
            high_points(1)
            for half in range(2):
                for n in units(half):
                    if n % NW == 0 and n // NW % NUH >= 1 and n // NW + 1 < 2 * NUH:
                        high_points(n // NW + 1)
                    act.wait_ge(segs_ready, n + 1)
                    if n >= 4:
                        act.wait_ge(weights_low, n - 3)
                    nc.scalar.activation(weights[:, n % 4, :], psum[:, 2 * (n % 4), :], ACT.Copy)\
                        .then_inc(first_out, 1)
                    if n > units(half)[0]:
                        high_weights(n - 1)
                    i = (n - Y_AT) // 2
                    if 0 <= i < B and (n - Y_AT) % 2 == 0:
                        batch = (slice(None), slice(None), slice(i * L, (i + 1) * L))
                        act.wait_ge(y_loaded[i // (B // 2)], 16 * B // 2)
                        nc.scalar.activation(r(y_h[batch]), y_l[batch], ACT.Copy).then_inc(y_high, 1)
                high_weights(units(half)[-1])
                if half == 0:
                    high_points(NUH + 1)
                with act.Fori(0, NTB) as b:
                    for it in range(ITH):
                        act.wait_ge(S["gate_ready"], at(half, b, "gate_ready", it + 1))
                        nc.scalar.activation(silu, psum[:, 4 + 2 * (it % 2), :], ACT.Silu)\
                            .then_inc(S["silu_out"], 1)
                        act.wait_ge(S["inter_out"], at(half, b, "inter_out", it + 1))
                        if it >= 2:
                            act.wait_ge(S["down_done"], at(half, b, "down_done", it - 1))
                        nc.scalar.activation(r(inter_h[:, it % 2, :]), inter, ACT.Copy)\
                            .then_inc(S["inter_high"], 1)

        @block.vector
        def _(dve):
            def low_weights(n):
                dve.wait_ge(weights_high, n + 1)
                nc.vector.tensor_tensor(r(w_l[n % NW][:, cols(n)]), weights[:, n % 4, :], w_h[n % NW][:, cols(n)],
                                        ALU.subtract).then_inc(weights_low, 1)

            dve.wait_ge(powers_high, 1)
            nc.vector.tensor_tensor(r(powers_l[:].rearrange("p a n -> p (a n)")), powers,
                                    powers_h[:].rearrange("p a n -> p (a n)"), ALU.subtract).then_inc(powers_low, 1)
            for half in range(2):
                dve.wait_ge(seg_loaded, 16 * (half + 1))
                for n in units(half):
                    dve.wait_ge(first_out, n + 1)
                    nc.vector.copy_predicated(weights[:, n % 4, :],
                                              seg[:, 1 if n % NW == 2 else 0, cols(n)],
                                              psum[:, 2 * (n % 4) + 1, :]).then_inc(second_out, 1)
                    if n > units(half)[0]:
                        low_weights(n - 1)
                    i = (n - Y_AT) // 2 - 1
                    if 0 <= i < B and (n - Y_AT) % 2 == 0:
                        batch = (slice(None), slice(None), slice(i * L, (i + 1) * L))
                        dve.wait_ge(y_high, i + 1)
                        nc.vector.tensor_tensor(r(y_l[batch]), y_l[batch], y_h[batch], ALU.subtract)\
                            .then_inc(y_low, 1)
                low_weights(units(half)[-1])
                with dve.Fori(0, NTB) as b:
                    def wait(name, count):
                        dve.wait_ge(S[name], at(half, b, name, count))

                    for it in range(ITH):
                        wait("silu_out", it + 1)
                        wait("up_ready", it + 1)
                        if it:
                            wait("inter_low", it)
                        nc.vector.tensor_tensor(inter, psum[:, 5 + 2 * (it % 2), :], silu, ALU.mult)\
                            .then_inc(S["inter_out"], 1)
                        wait("inter_high", it + 1)
                        nc.vector.tensor_tensor(r(inter_l[:, it % 2, :]), inter, inter_h[:, it % 2, :],
                                                ALU.subtract).then_inc(S["inter_low"], 1)
                    wait("down_done", ITH)
                    wait("xr_loaded", 16)
                    for s in range(ST):
                        nc.vector.tensor_tensor(x_res[:, s, :], psum[:, s, :], x_res[:, s, :], ALU.add)\
                            .then_inc(S["acc_out"], 1)


def block_program(nc, x_lanes, x_rows, taps, conv_b, qkv_wT, qk_b, v_b, out_wT, out_b, slopes, cond, w2T, att_b,
                  aug_consts, pos, ctrl, spline_m, spline_r, seg_mask, out):
    y_dram = nc.dram_tensor("y_scratch", (B, P, CT, L), F32, kind="Internal").ap()
    x1_dram = nc.dram_tensor("x1_scratch", (B, P, LT, D), F32, kind="Internal").ap()
    with nc.psum_tensor("psum", [P, 8, 512], F32) as psum:
        attention_part(nc, psum, y_dram, x1_dram, x_lanes, x_rows, taps, conv_b, qkv_wT, qk_b, v_b, out_wT,
                       out_b, slopes, cond, w2T, att_b, aug_consts, pos)
        feed_forward_part(nc, psum, y_dram, x1_dram, ctrl, spline_m, spline_r, seg_mask, out)


def spline_tables():
    import numpy as np
    n_samples = INTER * HIDDEN
    t = np.linspace(0.0, N_CTRL - 1.0, n_samples, dtype=np.float64)
    seg = np.clip(np.floor(t).astype(np.int64), 0, N_CTRL - 2).reshape(NRUN, P)
    start = seg[:, 0]
    frac = t.reshape(NRUN, P)[:, 0] - start
    step = (N_CTRL - 1.0) / (n_samples - 1)
    crossed = (seg != start[:, None]).astype(np.uint8)
    basis = 0.5 * np.array([[0, 2, 0, 0], [-1, 0, 1, 0], [2, -5, 4, -1], [-1, 3, -3, 1]], np.float64)
    binom = np.array([[1, 0, 0, 0], [1, 1, 0, 0], [1, 2, 1, 0], [1, 3, 3, 1]], np.float64)
    coefs = np.zeros((2, 4, 4, NRUN))
    for e in range(2):
        c = frac - e
        for j in range(4):
            for m in range(j, 4):
                coefs[e, j] += binom[m, j] * c[None, :] ** (m - j) * basis[m][:, None]
    powers = (np.arange(P)[None, :] * step) ** np.arange(4)[:, None]
    place = np.zeros((NW, 2, 4, 4, 2 * NW, P))
    for i in range(NW):
        for e in range(2):
            place[i, e, :, :, 2 * i + e, :] = powers[:, None, :]
    idx = np.zeros((2, 4, NRUN), np.int64)
    for e in range(2):
        for k in range(4):
            idx[e, k] = np.clip(start + e + k - 1, 0, N_CTRL - 1)
    runs = np.arange(NRUN)
    by_inner = runs.reshape(2, INTER // 2, CT).transpose(0, 2, 1).reshape(-1)
    by_outer = runs.reshape(HIDDEN, IT).T.reshape(-1)
    orders = (by_inner, by_inner, by_outer)
    rows = np.concatenate([coefs.reshape(32, NRUN)[:, o] for o in orders]).astype(np.float32)
    masks = np.stack([crossed[by_inner].T, crossed[by_outer].T], axis=1)
    masks = np.ascontiguousarray(masks.reshape(P, 2, 2, HALF).transpose(0, 2, 1, 3))
    picks = [np.broadcast_to(idx[:, None, :, o], (2, 4, 4, NRUN)).reshape(32, NRUN) for o in orders]
    return rows, place.reshape(NW * 32, 2 * NW * P).astype(np.float32), masks, picks


def kernel(**inputs):
    import numpy as np
    import concourse.bacc as bacc
    from concourse.bass_utils import run_bass_kernel_spmd

    a = {k: np.asarray(v) for k, v in inputs.items()}
    rows, powers, masks, picks = spline_tables()
    x = a["x"]
    cond = a["cond_2048"]
    late = np.concatenate([x[1:], x[:1]])
    qkv_w, qkv_b = a["L0_attn_qkv_w"], a["L0_attn_qkv_b"]
    points = np.concatenate([a[n][i] for n, i in zip(("L0_ffn_gate_cp", "L0_ffn_up_cp", "L0_ffn_down_cp"), picks)])
    arrays = {
        "x_lanes": late.transpose(0, 2, 1).reshape(B, CT, P, L).transpose(0, 2, 1, 3),
        "x_rows": late.reshape(B, LT, P, D).transpose(0, 2, 1, 3),
        "taps": cond.T,
        "conv_b": a["L0_cond_b"].reshape(CT, P).T,
        "qkv_wT": qkv_w.T,
        "qk_b": qkv_b[:2 * D].reshape(8, P).T,
        "v_b": qkv_b[2 * D:],
        "out_wT": a["L0_attn_out_w"].T,
        "out_b": a["L0_attn_out_b"],
        "slopes": a["L0_attn_alibi_slopes"].reshape(H1, 1),
        "cond": np.concatenate([cond[1:], cond[:1]]),
        "w2T": np.concatenate([a["L0_cond2_Wq"].T, a["L0_cond2_Wk"].T, a["L0_cond2_Wv"].T]),
        "att_b": a["L0_cond2_b"].reshape(1, 1),
        "aug_consts": np.array([[1, 0, 0], [-1, 1, NEG2]], np.float32),
        "pos": np.arange(L, dtype=np.float32),
        "ctrl": points,
        "spline_m": rows,
        "spline_r": powers,
        "seg_mask": masks.view(np.int32),
    }
    nc = bacc.Bacc("TRN2", target_bir_lowering=False, num_devices=1)
    args, feed = [], {}
    for name, v in arrays.items():
        v = np.ascontiguousarray(v)
        feed[f"in_{name}"] = v
        args.append(nc.dram_tensor(f"in_{name}", v.shape, mybir.dt.from_np(v.dtype), kind="ExternalInput").ap())
    out = nc.dram_tensor("out", (B, P, LT, D), F32, kind="ExternalOutput").ap()
    block_program(nc, *args, out)
    r = run_bass_kernel_spmd(nc, [feed], core_ids=[0])
    got = r.results[0]["out"]
    return got.transpose(0, 2, 1, 3).reshape(B, L, D)
```
